# Optimizing a Trainium2 kernel written in Bass

```python
import numpy as np
import jax
import jax.numpy as jnp

def _softmax(x, axis=-1):
    return jax.nn.softmax(x, axis=axis)

def _gelu(x):
    return jax.nn.gelu(x, approximate=True)

def _silu(x):
    return jax.nn.silu(x)

def _sigmoid(x):
    return jax.nn.sigmoid(x)

def _layernorm(x, axis=-1, eps=1e-05):
    m = jnp.mean(x, axis=axis, keepdims=True)
    v = jnp.var(x, axis=axis, keepdims=True)
    return (x - m) / jnp.sqrt(v + eps)

def _scatter_add(tgt, idx, src, axis=0):
    return tgt.at[idx].add(src)

def _segment_sum(src, seg, n):
    return jax.ops.segment_sum(src, seg, n)
kernel_name = 'mk_flamingo_gated_d1_seqx_r8_258e4e'

def setup_inputs(seed: int=0):
    np.random.seed(seed)
    _w = jnp.asarray

    def _rec_inputs():
        import jax
        import jax.numpy as jnp
        _rk = jax.random.key(seed)
        x = -0.0002928 + 1 * jax.random.normal(jax.random.fold_in(_rk, 1), (2, 512, 128), jnp.float32)
        _lenS = 512 - jax.random.randint(jax.random.fold_in(_rk, 7), (2,), 0, max(1, 512 // 4) + 1, jnp.int32)
        _lenS2 = 77 - jax.random.randint(jax.random.fold_in(_rk, 8), (2,), 0, max(1, 77 // 4) + 1, jnp.int32)
        _ctx_1024P = jax.random.normal(jax.random.fold_in(_rk, 11), (2, 16, 128), jnp.float32)
        _ctx_1024c = jax.random.dirichlet(jax.random.fold_in(_rk, 511), 0.3 * jnp.ones((16,), jnp.float32), (2, 77))
        _ctx_1024t = jnp.einsum('bsk,bkd->bsd', _ctx_1024c, _ctx_1024P)
        _ctx_1024t = _ctx_1024t * jax.lax.rsqrt(jnp.mean(jnp.square(_ctx_1024t)) + 1e-12) * 0.953939
        ctx_1024 = -1.52775e-05 + 0.999936 * (_ctx_1024t + 0.3 * jax.random.normal(jax.random.fold_in(_rk, 611), (2, 77, 128), jnp.float32))
        _g = jax.random.normal(jax.random.fold_in(_rk, 9001), (2, 1), jnp.float32)
        _g = jnp.sign(_g) * jnp.maximum(jnp.abs(_g), 1.0) + (_g == 0) * 1.0
        g_xattn = _g[0]
        g_ffn = _g[1]
        return (x, ctx_1024, g_xattn, g_ffn)
    x, ctx_1024, g_xattn, g_ffn = _rec_inputs()

    def _L0_xattn_setup():
        import jax, jax.numpy as jnp
        import numpy as np
        DIM = 128
        NUM_HEADS = 8
        HEAD_DIM = 64
        INNER = NUM_HEADS * HEAD_DIM
        key = jax.random.key(seed)
        ks = jax.random.split(key, 7)
        B, N, M = (8, 64, 512)
        x = jax.random.normal(ks[0], (B, N, DIM), dtype=jnp.float32)
        context = jax.random.normal(ks[1], (B, M, DIM), dtype=jnp.float32)
        s_in = 1.0 / np.sqrt(DIM)
        s_inner = 1.0 / np.sqrt(INNER)
        Wq = jax.random.normal(ks[2], (DIM, INNER), dtype=jnp.float32) * s_in
        Wk = jax.random.normal(ks[3], (DIM, INNER), dtype=jnp.float32) * s_in
        Wv = jax.random.normal(ks[4], (DIM, INNER), dtype=jnp.float32) * s_in
        Wo = jax.random.normal(ks[5], (INNER, DIM), dtype=jnp.float32) * s_inner
        bo = jax.random.normal(ks[6], (DIM,), dtype=jnp.float32) * 0.01
        return {'x': x, 'context': context, 'Wq': Wq, 'Wk': Wk, 'Wv': Wv, 'Wo': Wo, 'bo': bo}
    _L0_xattn_all = _L0_xattn_setup()
    _L0_xattn_in = {k: v for k, v in _L0_xattn_all.items() if k in ('Wq', 'Wk', 'Wv', 'Wo', 'bo')}
    del _L0_xattn_all

    def _L0_ffn_setup():
        import jax, jax.numpy as jnp
        import numpy as np
        D_MODEL = 128
        N_EXPERTS = 8
        TOP_K = 2
        FFN_HIDDEN = 4 * D_MODEL
        key = jax.random.key(seed)
        ks = jax.random.split(key, 6)

        def xavier(k, shape):
            fan_in, fan_out = (shape[-2], shape[-1])
            lim = jnp.sqrt(6.0 / (fan_in + fan_out))
            return jax.random.uniform(k, shape, jnp.float32, -lim, lim)
        x = jax.random.normal(ks[0], (4, 256, D_MODEL), jnp.float32)
        w_gate = xavier(ks[1], (N_EXPERTS, D_MODEL))
        W1 = xavier(ks[2], (N_EXPERTS, D_MODEL, FFN_HIDDEN))
        b1 = jnp.zeros((N_EXPERTS, FFN_HIDDEN), jnp.float32)
        W2 = xavier(ks[3], (N_EXPERTS, FFN_HIDDEN, D_MODEL))
        b2 = jnp.zeros((N_EXPERTS, D_MODEL), jnp.float32)
        return {'x': x, 'w_gate': w_gate, 'W1': W1, 'b1': b1, 'W2': W2, 'b2': b2}
    _L0_ffn_all = _L0_ffn_setup()
    _L0_ffn_in = {k: v for k, v in _L0_ffn_all.items() if k in ('w_gate', 'W1', 'b1', 'W2', 'b2')}
    del _L0_ffn_all
    return {'x': x, 'ctx_1024': ctx_1024, 'g_xattn': g_xattn, 'g_ffn': g_ffn, 'L0_xattn_Wq': _L0_xattn_in['Wq'], 'L0_xattn_Wk': _L0_xattn_in['Wk'], 'L0_xattn_Wv': _L0_xattn_in['Wv'], 'L0_xattn_Wo': _L0_xattn_in['Wo'], 'L0_xattn_bo': _L0_xattn_in['bo'], 'L0_ffn_w_gate': _L0_ffn_in['w_gate'], 'L0_ffn_W1': _L0_ffn_in['W1'], 'L0_ffn_b1': _L0_ffn_in['b1'], 'L0_ffn_W2': _L0_ffn_in['W2'], 'L0_ffn_b2': _L0_ffn_in['b2']}

def reference(x, ctx_1024, g_xattn, g_ffn, L0_xattn_Wq, L0_xattn_Wk, L0_xattn_Wv, L0_xattn_Wo, L0_xattn_bo, L0_ffn_w_gate, L0_ffn_W1, L0_ffn_b1, L0_ffn_W2, L0_ffn_b2):
    import jax
    import jax.numpy as jnp

    def _L0_xattn_ref(x, context, Wq, Wk, Wv, Wo, bo):
        import jax, jax.numpy as jnp
        import numpy as np
        DIM = 128
        NUM_HEADS = 8
        HEAD_DIM = 64
        INNER = NUM_HEADS * HEAD_DIM
        B, N, _ = x.shape
        M = context.shape[1]
        scale = HEAD_DIM ** (-0.5)
        q = (x @ Wq).reshape(B, N, NUM_HEADS, HEAD_DIM).transpose(0, 2, 1, 3)
        k = (context @ Wk).reshape(B, M, NUM_HEADS, HEAD_DIM).transpose(0, 2, 1, 3)
        v = (context @ Wv).reshape(B, M, NUM_HEADS, HEAD_DIM).transpose(0, 2, 1, 3)
        attn = jax.nn.softmax(jnp.einsum('bhnd,bhmd->bhnm', q, k) * scale, axis=-1)
        out = jnp.einsum('bhnm,bhmd->bhnd', attn, v)
        out = out.transpose(0, 2, 1, 3).reshape(B, N, INNER)
        return out @ Wo + bo

    def _L0_ffn_ref(x, w_gate, W1, b1, W2, b2):
        import jax, jax.numpy as jnp
        import numpy as np
        D_MODEL = 128
        N_EXPERTS = 8
        TOP_K = 2
        FFN_HIDDEN = 4 * D_MODEL
        B, S, D = x.shape
        flat_x = x.reshape(-1, D)
        gate = jax.nn.softmax(flat_x @ w_gate.T, axis=-1)
        topk_scores, topk_idx = jax.lax.top_k(gate, TOP_K)
        cw = (jax.nn.one_hot(topk_idx, N_EXPERTS, dtype=flat_x.dtype) * topk_scores[..., None]).sum(axis=1)
        h = jax.nn.gelu(jnp.einsum('td,edh->teh', flat_x, W1) + b1, approximate=False)
        y = jnp.einsum('teh,ehd->ted', h, W2) + b2
        out = jnp.einsum('ted,te->td', y, cw)
        return out.reshape(B, S, D)
    x = x + jnp.tanh(g_xattn[0]) * _L0_xattn_ref(_layernorm(x, axis=-1), ctx_1024, L0_xattn_Wq, L0_xattn_Wk, L0_xattn_Wv, L0_xattn_Wo, L0_xattn_bo)
    x = x + jnp.tanh(g_ffn[0]) * _L0_ffn_ref(_layernorm(x, axis=-1), L0_ffn_w_gate, L0_ffn_W1, L0_ffn_b1, L0_ffn_W2, L0_ffn_b2)
    return x

_drawn_inputs = setup_inputs


def setup_inputs(seed=0):
    import zlib

    import numpy as np

    out = dict(_drawn_inputs(seed))
    spreads = {'L0_ffn_b1': (0.0, 0.1), 'L0_ffn_b2': (0.0, 0.1)}
    factors = {'L0_xattn_bo': 4.305}
    for name, (base, spread) in spreads.items():
        noise = np.random.default_rng([zlib.crc32(name.encode()), seed]).standard_normal(out[name].shape)
        drawn = base * np.exp(spread * noise) if base else spread * noise
        out[name] = jnp.asarray(drawn.astype(out[name].dtype))
    for name, factor in factors.items():
        out[name] = (out[name] * factor).astype(out[name].dtype)
    return out
```

```python
from contextlib import ExitStack

import concourse.bass as bass
from concourse import mybir

F32 = mybir.dt.float32
F32R = mybir.dt.float32r
ALU = mybir.AluOpType
ACT = mybir.ActivationFunctionType
AX_X = mybir.AxisListType.X

P = 128
HEADS = 8
EPS = 1e-5
JUNK = -3.0e38
FOUND = 3.0e38
EULER = 2.718281828459045


def flamingo_block(nc, x, ctx_in, g_xattn, g_ffn, Wq, Wk, Wv, Wo, bo, w_gate, W1, b1, W2, b2, out):
    B, S, D = x.shape
    M = ctx_in.shape[1]
    INNER = Wq.shape[1]
    HD = INNER // HEADS
    E, _, HID = W1.shape
    assert D == P and HD == 64 and E == 8 and HID % P == 0 and S % P == 0
    NT = S // P
    T = B * NT
    J = INNER // P
    HM = HEADS * M
    HH = HM // 2
    CH = -(-HM // P)
    HMP = CH * P
    MT = HID // P
    STEPS = E * B
    G = STEPS * MT
    LAG = 3
    PAIRS = E // 2
    PT_TILES = 2 * B * MT
    BW = 2 * P

    with ExitStack() as stack:
        def sb(name, shape, dt=F32):
            return stack.enter_context(nc.sbuf_tensor(name, shape, dt))

        def sem(name):
            return stack.enter_context(nc.semaphore(name))

        psum = stack.enter_context(nc.psum_tensor("psum", [P, 8, 512], F32))
        psum_flat = psum[:, :, :].rearrange("p b n -> p (b n)")

        x_sb = sb("x_sb", [P, B, NT, D])
        ctx_sb = sb("ctx_sb", [M, B, D])
        wq_sb = sb("wq_sb", [P, INNER])
        wk_sb = sb("wk_sb", [P, INNER])
        wv_sb = sb("wv_sb", [P, INNER])
        wo_sb = sb("wo_sb", [P, J, D])
        bo_sb = sb("bo_sb", [P, D])
        gates_in = sb("gates_in", [P, 2])
        wg_sb = sb("wg_sb", [E, D])
        b1_sb = sb("b1_sb", [E * MT, P])
        b2_sb = sb("b2_sb", [2 * E, D])
        w1_sb = sb("w1_sb", [P, E, HID])
        w2_sb = sb("w2_sb", [P, E, MT, D])
        ident = sb("ident", [P, P])
        minus_half = sb("minus_half", [P, T])
        euler = sb("euler", [P, NT, E])
        sel_f = sb("sel_f", [2 * E, E, P])
        tanh_g = sb("tanh_g", [P, 2])
        tbo = sb("tbo", [P, D])
        wqT = sb("wqT", [P, J, D])
        ctxT = sb("ctxT", [P, B * M])
        kT = sb("kT", [P, J, B * M])
        v_blocks = sb("v_blocks", [P, B * J * BW + BW])
        a_hi = sb("a_hi", [P, B, HEADS, M], F32R)
        a_lo = sb("a_lo", [P, B, HEADS, M], F32R)
        vo_hi = sb("vo_hi", [P, B * CH, D], F32R)
        vo_lo = sb("vo_lo", [P, B * CH, D], F32R)
        wg_hi = sb("wg_hi", [P, E], F32R)
        wg_lo = sb("wg_lo", [P, E], F32R)
        b1T = sb("b1T", [P, E * MT])
        b2_hi = sb("b2_hi", [2 * E, D], F32R)
        b2_lo = sb("b2_lo", [2 * E, D], F32R)
        bn1 = sb("bn1", [P, T, 6])
        mv1 = sb("mv1", [P, T, 2])
        ve1 = sb("ve1", [P, T])
        rstd1 = sb("rstd1", [P, T])
        xb = sb("xb", [P, T, D])
        xn1 = sb("xn1", [P, T, D])
        xnT_hi = [sb(f"xnT_hi{u}", [P, P], F32R) for u in range(2)]
        xnT_lo = [sb(f"xnT_lo{u}", [P, P], F32R) for u in range(2)]
        smax = sb("smax", [P, 2, HEADS])
        ssum = sb("ssum", [P, 2, HEADS])
        srec = sb("srec", [P, 2, HEADS])
        prob = sb("prob", [P, 2, HMP])
        pT_hi = [sb(f"pT_hi{u}", [P, HMP], F32R) for u in range(2)]
        pT_lo = [sb(f"pT_lo{u}", [P, HMP], F32R) for u in range(2)]
        x1 = sb("x1", [P, T, D])
        bn2 = sb("bn2", [P, T, 6])
        mv2 = sb("mv2", [P, T, 2])
        ve2 = sb("ve2", [P, T])
        rstd2 = sb("rstd2", [P, T])
        xn2 = sb("xn2", [P, T, D])
        x2_hi = sb("x2_hi", [P, T, P], F32R)
        x2_lo = sb("x2_lo", [P, T, P], F32R)
        logit = sb("logit", [P, B, NT, E + 6])
        top8 = sb("top8", [P, B, NT, 8])
        best = sb("best", [P, B, NT, 8])
        found = sb("found", [P, B, NT, E + 6])
        gd = sb("gd", [P, B, NT, E])
        gexp = sb("gexp", [P, B, NT, E])
        gsum = sb("gsum", [P, B, NT])
        grec = sb("grec", [P, B, NT])
        gscale = sb("gscale", [P, B, NT])
        gpick = sb("gpick", [P, B, NT, E])
        cw = sb("cw", [P, B, NT, E])
        cw_hl = sb("cw_hl", [P, B, NT, 2 * E], F32R)
        cwT = sb("cwT", [2 * E, B, S], F32R)
        b1_e = [sb(f"b1_e{u}", [P, MT]) for u in range(2)]
        sel_e = [sb(f"sel_e{u}", [2 * E, P], F32R) for u in range(2)]
        cwb = sb("cwb", [P, B, S])
        w1_hi = [sb(f"w1_hi{u}", [P, HID], F32R) for u in range(2)]
        w1_lo = [sb(f"w1_lo{u}", [P, HID], F32R) for u in range(2)]
        w2_hi = [sb(f"w2_hi{u}", [P, MT, D], F32R) for u in range(2)]
        w2_lo = [sb(f"w2_lo{u}", [P, MT, D], F32R) for u in range(2)]
        g_hi = sb("g_hi", [P, 4, S], F32R)
        g_lo = sb("g_lo", [P, 4, S], F32R)
        y_cw = sb("y_cw", [P, 2, S])
        acc = sb("acc", [P, B, S])
        fin = sb("fin", [P, B, NT * D])

        SC = psum[:, 0:2, 0:HH].rearrange("p b (h m) -> p b h m", m=M)
        PT = psum_flat[:, 2 * 512:2 * 512 + HMP]
        AO = psum[:, 4, 0:D]
        XT1 = psum[:, 5, 0:P]
        XT2 = psum[:, 6, 0:P]
        GATE_BANKS, CWT_BANK, B2_BANK = (7, 6), 5, 4
        Y_BANKS, CWB_BANKS, FIN_BANKS = (4, 5), (6, 7), (6, 7)

        d_ctx, d_wq, d_wk, d_wv, d_wo = sem("d_ctx"), sem("d_wq"), sem("d_wk"), sem("d_wv"), sem("d_wo")
        d_x = [sem(f"d_x{b}") for b in range(B)]
        d_bo, d_g, d_wg, d_b1, d_b2 = sem("d_bo"), sem("d_g"), sem("d_wg"), sem("d_b1"), sem("d_b2")
        d_w1 = [sem(f"d_w1_{i}") for i in range(2)]
        d_w2 = [sem(f"d_w2_{i}") for i in range(2)]
        d_out = sem("d_out")
        ident_zero, ident_done = sem("ident_zero"), sem("ident_done")
        consts_done, sel_zero, sel_steps, sel_done = sem("consts_done"), sem("sel_zero"), sem("sel_steps"), sem("sel_done")
        vzero_done = sem("vzero_done")
        wqT_ps, wqT_done = sem("wqT_ps"), sem("wqT_done")
        ctxT_ps, ctxT_done = sem("ctxT_ps"), sem("ctxT_done")
        small_ps, small_done = sem("small_ps"), sem("small_done")
        wg_hi_done, wg_lo_done, b2_hi_done, b2_lo_done = sem("wg_hi_done"), sem("wg_lo_done"), sem("b2_hi_done"), sem("b2_lo_done")
        kT_ps, kT_done, vT_ps, v_done = sem("kT_ps"), sem("kT_done"), sem("vT_ps"), sem("v_done")
        a_ps, a_hi_done, a_lo_done = sem("a_ps"), sem("a_hi_done"), sem("a_lo_done")
        vo_ps, vo_hi_done, vo_lo_done = sem("vo_ps"), sem("vo_hi_done"), sem("vo_lo_done")
        tanh_done, tbo_done, xb_done = sem("tanh_done"), sem("tbo_done"), sem("xb_done")
        bn1_done, mv1_done, ve1_done, rstd1_done, xn1_done = sem("bn1_done"), sem("mv1_done"), sem("ve1_done"), sem("rstd1_done"), sem("xn1_done")
        xT1_ps, xT1_hi_done, xT1_lo_done = sem("xT1_ps"), sem("xT1_hi_done"), sem("xT1_lo_done")
        sc_ps, smax_done, ssub_done, exp_done = sem("sc_ps"), sem("smax_done"), sem("ssub_done"), sem("exp_done")
        ssum_done, srec_done, norm_done = sem("ssum_done"), sem("srec_done"), sem("norm_done")
        pT_ps, pT_hi_done, pT_lo_done = sem("pT_ps"), sem("pT_hi_done"), sem("pT_lo_done")
        ao_ps, x1_done, bn2_done, mv2_done = sem("ao_ps"), sem("x1_done"), sem("bn2_done"), sem("mv2_done")
        ve2_done, rstd2_done, xn2_done = sem("ve2_done"), sem("rstd2_done"), sem("xn2_done")
        xT2_ps, x2_hi_done, x2_lo_done = sem("xT2_ps"), sem("x2_hi_done"), sem("x2_lo_done")
        gate_ps, logit_done, top8_done, best_done = sem("gate_ps"), sem("logit_done"), sem("top8_done"), sem("best_done")
        found_done, gd_done, gexp_done, gsum_done = sem("found_done"), sem("gd_done"), sem("gexp_done"), sem("gsum_done")
        grec_done, gscale_done, gpick_done, cw_done = sem("grec_done"), sem("gscale_done"), sem("gpick_done"), sem("cw_done")
        cw_hi_done, cw_lo_done, cwT_ps, cwT_done = sem("cw_hi_done"), sem("cw_lo_done"), sem("cwT_ps"), sem("cwT_done")
        cwb_ps, cwb_done, b2_ps, acc_init = sem("cwb_ps"), sem("cwb_done"), sem("b2_ps"), sem("acc_init")
        w_hi_done, w_hi_seen, w_split = sem("w_hi_done"), sem("w_hi_seen"), sem("w_split")
        h_ps, gelu_done, g_hi_done, g_lo_done = sem("h_ps"), sem("gelu_done"), sem("g_hi_done"), sem("g_lo_done")
        y_ps, y_cw_done, acc_done = sem("y_ps"), sem("y_cw_done"), sem("acc_done")
        fin_ps, fin_done = sem("fin_ps"), sem("fin_done")

        def a_psum(bank):
            return psum[:, bank, 0:2 * B * M].rearrange("p (c b m) -> p b c m", c=2, b=B)

        def a_view(t, bank):
            first = 4 * (bank % 2) + bank // 2
            return t[:, :, first:first + 3:2, :]

        VO_BANKS = (4, 6, 7)

        def vo_psum(q):
            n = min(4, B * CH - 4 * q)
            return psum[:, VO_BANKS[q], 0:n * D].rearrange("p (c d) -> p c d", d=D)

        def vo_view(t, q):
            return t[:, 4 * q:min(4 * q + 4, B * CH), :]

        block = stack.enter_context(nc.Block())

        @block.sync
        def _(sp):
            sp.dma_start(ctx_sb[:, :, :], ctx_in.rearrange("b m d -> m b d")).then_inc(d_ctx, 16)
            sp.dma_start(wk_sb[:, :], Wk).then_inc(d_wk, 16)
            sp.dma_start(x_sb[:, 0, :, :], x[0].rearrange("(p n) d -> p n d", n=NT)).then_inc(d_x[0], 16)
            sp.dma_start(wv_sb[:, :], Wv).then_inc(d_wv, 16)
            sp.dma_start(x_sb[:, 1, :, :], x[1].rearrange("(p n) d -> p n d", n=NT)).then_inc(d_x[1], 16)
            sp.dma_start(wo_sb[:, :, :], Wo.rearrange("(j p) d -> p j d", p=P)).then_inc(d_wo, 16)
            for i in range(2):
                half = slice(i * E // 2, (i + 1) * E // 2)
                sp.dma_start(w1_sb[:, half, :], W1[half].rearrange("e d h -> d e h")).then_inc(d_w1[i], 16)
                for e in range(i * E // 2, (i + 1) * E // 2):
                    sp.dma_start(w2_sb[:, e, :, :], W2[e].rearrange("(k p) d -> p k d", p=P)).then_inc(d_w2[i], 16)
            for b in range(B):
                sp.wait_ge(fin_done, b + 1)
                sp.dma_start(out[b].rearrange("(p n) d -> p (n d)", n=NT), fin[:, b, :]).then_inc(d_out, 16)
            sp.wait_ge(d_out, 16 * B)

        @block.gpsimd
        def _(pool):
            nc.gpsimd.memset(ident[:, :], 0.0).then_inc(ident_zero, 1)
            pool.wait_ge(ident_zero, 1)
            nc.gpsimd.affine_select(out=ident[:, :], in_=ident[:, :], compare_op=ALU.not_equal, fill=1.0, base=0,
                                    pattern=[[-1, P]], channel_multiplier=1).then_inc(ident_done, 1)
            pool.dma_start(gates_in[:, 0:1], g_xattn.partition_broadcast(P)).then_inc(d_g, 16)
            pool.dma_start(gates_in[:, 1:2], g_ffn.partition_broadcast(P)).then_inc(d_g, 16)
            pool.dma_start(bo_sb[:, :], bo.partition_broadcast(P)).then_inc(d_bo, 16)
            pool.dma_start(wg_sb[:, :], w_gate).then_inc(d_wg, 16)
            pool.dma_start(b1_sb[:, :], b1.rearrange("e (m p) -> (e m) p", p=P)).then_inc(d_b1, 16)
            for half in range(2):
                pool.dma_start(b2_sb[half * E:(half + 1) * E, :], b2).then_inc(d_b2, 16)
            nc.gpsimd.memset(v_blocks[:, :], 0.0).then_inc(vzero_done, 1)
            nc.gpsimd.memset(minus_half[:, :], -0.5).then_inc(consts_done, 1)
            nc.gpsimd.memset(euler[:, :, :], EULER).then_inc(consts_done, 1)
            nc.gpsimd.memset(prob[:, :, HM:HMP], 0.0).then_inc(consts_done, 1)
            nc.gpsimd.memset(logit[:, :, :, E:E + 6], JUNK).then_inc(consts_done, 1)
            nc.gpsimd.memset(best[:, :, :, 2:8], JUNK).then_inc(consts_done, 1)
            for b in range(B):
                tiles = slice(b * NT, (b + 1) * NT)
                pool.wait_ge(mv1_done, (b + 1) * NT)
                nc.gpsimd.tensor_scalar(ve1[:, tiles], mv1[:, tiles, 1], EPS, None, ALU.add).then_inc(ve1_done, 1)
                pool.wait_ge(ve1_done, b + 1)
                if b == 0:
                    pool.wait_ge(consts_done, 5)
                nc.gpsimd.tensor_tensor(rstd1[:, tiles], ve1[:, tiles], minus_half[:, tiles], ALU.pow).then_inc(rstd1_done, 1)
            nc.gpsimd.memset(sel_f[:, :, :], 0.0).then_inc(sel_zero, 1)
            pool.wait_ge(sel_zero, 1)
            for half in range(2):
                nc.gpsimd.affine_select(out=sel_f[:, :, :], in_=sel_f[:, :, :], compare_op=ALU.not_equal, fill=1.0,
                                        base=-half * E, pattern=[[-1, E], [0, P]], channel_multiplier=1).then_inc(sel_steps, 1)
                pool.wait_ge(sel_steps, half + 1)
            pool.wait_ge(d_bo, 16)
            pool.wait_ge(tanh_done, 1)
            nc.gpsimd.tensor_scalar(tbo[:, :], bo_sb[:, :], tanh_g[:, 0:1], None, ALU.mult).then_inc(tbo_done, 1)
            pool.wait_ge(tbo_done, 1)
            for b in range(B):
                pool.wait_ge(d_x[b], 16)
                nc.gpsimd.tensor_tensor(xb[:, b * NT:(b + 1) * NT, :], x_sb[:, b, :, :],
                                        tbo[:, :].unsqueeze(1).to_broadcast([P, NT, D]), ALU.add).then_inc(xb_done, 1)

            def split_expert(e, u):
                pool.wait_ge(small_done, 1)
                nc.gpsimd.tensor_copy(b1_e[u][:, :], b1T[:, bass.ds(e * MT, MT)]).then_inc(w_split, 1)
                nc.gpsimd.tensor_copy(w1_hi[u][:, :], w1_sb[:, e, :]).then_inc(w_hi_done, 1)
                nc.gpsimd.tensor_copy(w2_hi[u][:, :, :], w2_sb[:, e, :, :]).then_inc(w_hi_done, 1)
                nc.gpsimd.tensor_copy(sel_e[u][:, :], sel_f[:, e, :]).then_inc(w_split, 1)
                pool.wait_ge(w_hi_done, 2 * e + 2)
                pool.sem_inc(w_hi_seen, 1)
                nc.gpsimd.tensor_tensor(w1_lo[u][:, :], w1_sb[:, e, :], w1_hi[u][:, :].bitcast(F32), ALU.subtract).then_inc(w_split, 1)
                nc.gpsimd.tensor_tensor(w2_lo[u][:, :, :], w2_sb[:, e, :, :], w2_hi[u][:, :, :].bitcast(F32), ALU.subtract).then_inc(w_split, 1)

            for k in range(T + 1):
                if k < T:
                    pool.wait_ge(srec_done, k + 1)
                    p_k = prob[:, k % 2, 0:HM].rearrange("p (h m) -> p h m", m=M)
                    nc.gpsimd.tensor_tensor(p_k, p_k, srec[:, k % 2, :].unsqueeze(2).to_broadcast([P, HEADS, M]),
                                            ALU.mult).then_inc(norm_done, 1)
                if k >= 1:
                    pool.wait_ge(mv2_done, k)
                    nc.gpsimd.tensor_scalar(ve2[:, k - 1:k], mv2[:, k - 1, 1:2], EPS, None, ALU.add).then_inc(ve2_done, 1)
                    pool.wait_ge(ve2_done, k)
                    nc.gpsimd.tensor_tensor(rstd2[:, k - 1:k], ve2[:, k - 1:k], minus_half[:, 0:1], ALU.pow).then_inc(rstd2_done, 1)
                if k == T // 2:
                    pool.wait_ge(d_w1[0], 16)
                    pool.wait_ge(d_w2[0], 16 * (E // 2))
                    split_expert(0, 0)
            for b in range(B):
                pool.wait_ge(gd_done, b + 1)
                nc.gpsimd.tensor_tensor(gexp[:, b, :, :], euler[:, :, :], gd[:, b, :, :], ALU.pow).then_inc(gexp_done, 1)
            pool.wait_ge(d_w1[1], 16)
            pool.wait_ge(d_w2[1], 16 * (E // 2))

            def add_y(s, b):
                pool.wait_ge(y_cw_done, s + 1)
                if isinstance(s, int) and s < B:
                    pool.wait_ge(acc_init, B)
                else:
                    pool.wait_ge(acc_done, s - 1)
                nc.gpsimd.tensor_tensor(acc[:, b, :], acc[:, b, :], y_cw[:, b, :], ALU.add).then_inc(acc_done, 1)

            def expert(e, u, first=False, last=False):
                if not first:
                    add_y(B * e - 1, 1)
                if not last:
                    if not first:
                        pool.wait_ge(y_ps, B * e)
                    split_expert(e + 1, 1 - u)
                add_y(B * e, 0)

            expert(0, 0, first=True)
            expert(1, 1)
            with pool.Fori(1, PAIRS - 1) as i:
                expert(2 * i, 0)
                expert(2 * i + 1, 1)
            expert(E - 2, 0)
            expert(E - 1, 1, last=True)
            add_y(STEPS - 1, 1)

        @block.scalar
        def _(act):
            act.dma_start(wq_sb[:, :], Wq).then_inc(d_wq, 16)
            act.wait_ge(d_g, 32)
            nc.scalar.activation(tanh_g[:, :], gates_in[:, :], ACT.Tanh).then_inc(tanh_done, 1)
            act.wait_ge(ctxT_ps, 1)
            nc.scalar.copy(ctxT[:, :], psum[:, 7, 0:B * M]).then_inc(ctxT_done, 1)
            for q in range(2):
                act.wait_ge(kT_ps, q + 1)
                nc.scalar.activation(kT[:, 2 * q:2 * q + 2, :], psum[:, q, 0:2 * B * M].rearrange("p (c n) -> p c n", c=2),
                                     ACT.Copy, scale=HD ** -0.5).then_inc(kT_done, 1)
            for bank in range(4):
                act.wait_ge(a_ps, bank + 1)
                nc.scalar.copy(a_view(a_hi, bank), a_psum(bank)).then_inc(a_hi_done, 1)
            act.wait_ge(small_ps, 1)
            nc.scalar.copy(wg_hi[:, :], psum[:, 7, 320:320 + E]).then_inc(wg_hi_done, 1)
            nc.scalar.copy(b1T[:, :], psum[:, 7, 352:352 + E * MT]).then_inc(small_done, 1)

            def xT1_hi(k):
                act.wait_ge(xT1_ps, k + 1)
                if k >= 2:
                    act.wait_ge(sc_ps, k - 1)
                nc.scalar.copy(xnT_hi[k % 2][:, :], XT1).then_inc(xT1_hi_done, 1)

            xT1_hi(0)
            xT1_hi(1)
            act.wait_ge(d_b2, 32)
            nc.scalar.copy(b2_hi[:, :], b2_sb[:, :]).then_inc(b2_hi_done, 1)
            for q in range(3):
                act.wait_ge(vo_ps, q + 1)
                nc.scalar.copy(vo_view(vo_hi, q), vo_psum(q)).then_inc(vo_hi_done, 1)

            for k in range(T + 2):
                if k < T:
                    act.wait_ge(ssub_done, k + 1)
                    nc.scalar.activation(prob[:, k % 2, 0:HM], prob[:, k % 2, 0:HM], ACT.Exp).then_inc(exp_done, 1)
                if k + 2 < T:
                    xT1_hi(k + 2)
                if k >= 2:
                    act.wait_ge(xT2_ps, k - 1)
                    nc.scalar.copy(x2_hi[:, k - 2, :], XT2).then_inc(x2_hi_done, 1)
                if k < T:
                    act.wait_ge(pT_ps, k + 1)
                    if k >= 2:
                        act.wait_ge(ao_ps, k - 1)
                    nc.scalar.copy(pT_hi[k % 2][:, :], PT).then_inc(pT_hi_done, 1)

            def pair(i, first=False):
                for j in range(PT_TILES):
                    g, s, u, b, m = PT_TILES * i + j, 2 * B * i + j // MT, j // (B * MT), j // MT % B, j % MT
                    act.wait_ge(h_ps, g + 1)
                    nc.scalar.activation(psum[:, j % 4, :], psum[:, j % 4, :], ACT.Gelu,
                                         bias=b1_e[u][:, m:m + 1]).then_inc(gelu_done, 1)
                    if not (first and j == 0):
                        act.wait_ge(gelu_done, g)
                        nc.scalar.copy(g_hi[:, (j - 1) % 4, :], psum[:, (j - 1) % 4, :]).then_inc(g_hi_done, 1)
                    if first and j == 2:
                        for bb in range(B):
                            act.wait_ge(b2_ps, bb + 1)
                            nc.scalar.copy(acc[:, bb, :], psum[:, B2_BANK, :]).then_inc(acc_init, 1)
                    if m == MT - 1:
                        act.wait_ge(cwb_ps, s + 1)
                        if not (first and j < B * MT):
                            act.wait_ge(y_cw_done, s - 1)
                        nc.scalar.copy(cwb[:, b, :], psum[:, CWB_BANKS[b], :]).then_inc(cwb_done, 1)

            pair(0, first=True)
            with act.Fori(1, PAIRS) as i:
                pair(i)
            act.wait_ge(gelu_done, G)
            nc.scalar.copy(g_hi[:, 3, :], psum[:, 3, :]).then_inc(g_hi_done, 1)

        @block.vector
        def _(dve):
            def stats1(b):
                dve.wait_ge(d_x[b], 16)
                for t in range(b * NT, (b + 1) * NT):
                    nc.vector.bn_stats(bn1[:, t, :], x_sb[:, b, t % NT, :]).then_inc(bn1_done, 1)
                for t in range(b * NT, (b + 1) * NT):
                    dve.wait_ge(bn1_done, t + 1)
                    nc.vector.bn_aggr(mv1[:, t, :], bn1[:, t, :]).then_inc(mv1_done, 1)

            def normalise1(b):
                dve.wait_ge(rstd1_done, b + 1)
                for t in range(b * NT, (b + 1) * NT):
                    nc.vector.tensor_scalar(xn1[:, t, :], x_sb[:, b, t % NT, :], mv1[:, t, 0:1], rstd1[:, t:t + 1],
                                            ALU.subtract, ALU.mult).then_inc(xn1_done, 1)

            def xT1_lo(k):
                dve.wait_ge(xT1_hi_done, k + 1)
                nc.vector.tensor_tensor(xnT_lo[k % 2][:, :], XT1, xnT_hi[k % 2][:, :].bitcast(F32),
                                        ALU.subtract).then_inc(xT1_lo_done, 1)

            stats1(0)
            dve.wait_ge(wqT_ps, 1)
            nc.vector.tensor_copy(wqT[:, :, :], psum[:, 6, 0:J * D].rearrange("p (j d) -> p j d", j=J)).then_inc(wqT_done, 1)
            normalise1(0)
            dve.wait_ge(vzero_done, 1)
            dve.wait_ge(vT_ps, 2)
            for b in range(B):
                for par in range(2):
                    rows = slice(par * HD, (par + 1) * HD)
                    at = b * J * BW + par * M
                    stride = BW + 2 * M - P
                    dst = v_blocks[rows, at:at + J * stride].rearrange("p (j c) -> p j c", c=stride)[:, :, 0:M]
                    for half in range(2):
                        src = psum[rows, 2 + half, 0:2 * B * M].rearrange("p (c b m) -> p c b m", c=2, b=B)
                        nc.vector.tensor_copy(dst[:, 2 * half:2 * half + 2, :], src[:, :, b, :]).then_inc(v_done, 1)
            for bank in range(4):
                dve.wait_ge(a_hi_done, bank + 1)
                nc.vector.tensor_tensor(a_view(a_lo, bank), a_psum(bank), a_view(a_hi, bank).bitcast(F32),
                                        ALU.subtract).then_inc(a_lo_done, 1)
            xT1_lo(0)
            stats1(1)
            xT1_lo(1)
            normalise1(1)
            dve.wait_ge(wg_hi_done, 1)
            nc.vector.tensor_tensor(wg_lo[:, :], psum[:, 7, 320:320 + E], wg_hi[:, :].bitcast(F32), ALU.subtract).then_inc(wg_lo_done, 1)
            dve.wait_ge(b2_hi_done, 1)
            nc.vector.tensor_tensor(b2_lo[:, :], b2_sb[:, :], b2_hi[:, :].bitcast(F32), ALU.subtract).then_inc(b2_lo_done, 1)
            for q in range(3):
                dve.wait_ge(vo_hi_done, q + 1)
                nc.vector.tensor_tensor(vo_view(vo_lo, q), vo_psum(q), vo_view(vo_hi, q).bitcast(F32),
                                        ALU.subtract).then_inc(vo_lo_done, 1)

            for k in range(T + 3):
                if k < T:
                    dve.wait_ge(sc_ps, k + 1)
                    max_k = smax[:, k % 2, :].rearrange("p (b h) -> p b h", b=2)
                    nc.vector.tensor_reduce(max_k, SC, AX_X, ALU.max).then_inc(smax_done, 1)
                    dve.wait_ge(smax_done, k + 1)
                    if k >= 2:
                        dve.wait_ge(pT_ps, k - 1)
                    else:
                        dve.wait_ge(consts_done, 5)
                    nc.vector.tensor_tensor(prob[:, k % 2, 0:HM].rearrange("p (b h m) -> p b h m", b=2, m=M), SC,
                                            max_k.unsqueeze(3).to_broadcast([P, 2, HEADS // 2, M]),
                                            ALU.subtract).then_inc(ssub_done, 1)
                if 1 <= k <= T:
                    dve.wait_ge(pT_hi_done, k)
                    if k >= 3:
                        dve.wait_ge(ao_ps, k - 2)
                    nc.vector.tensor_tensor(pT_lo[(k - 1) % 2][:, :], PT, pT_hi[(k - 1) % 2][:, :].bitcast(F32),
                                            ALU.subtract).then_inc(pT_lo_done, 1)
                if k < T:
                    dve.wait_ge(exp_done, k + 1)
                    nc.vector.tensor_reduce(ssum[:, k % 2, :], prob[:, k % 2, 0:HM].rearrange("p (h m) -> p h m", m=M),
                                            AX_X, ALU.add).then_inc(ssum_done, 1)
                    dve.wait_ge(ssum_done, k + 1)
                    nc.vector.reciprocal(srec[:, k % 2, :], ssum[:, k % 2, :]).then_inc(srec_done, 1)
                if k + 2 < T:
                    xT1_lo(k + 2)
                if 1 <= k <= T:
                    dve.wait_ge(ao_ps, k)
                    dve.wait_ge(xb_done, (k - 1) // NT + 1)
                    nc.vector.scalar_tensor_tensor(x1[:, k - 1, :], AO, tanh_g[:, 0:1], xb[:, k - 1, :],
                                                   ALU.mult, ALU.add).then_inc(x1_done, 1)
                    dve.wait_ge(x1_done, k)
                    nc.vector.bn_stats(bn2[:, k - 1, :], x1[:, k - 1, :]).then_inc(bn2_done, 1)
                    dve.wait_ge(bn2_done, k)
                    nc.vector.bn_aggr(mv2[:, k - 1, :], bn2[:, k - 1, :]).then_inc(mv2_done, 1)
                if 2 <= k <= T + 1:
                    dve.wait_ge(rstd2_done, k - 1)
                    nc.vector.tensor_scalar(xn2[:, k - 2, :], x1[:, k - 2, :], mv2[:, k - 2, 0:1], rstd2[:, k - 2:k - 1],
                                            ALU.subtract, ALU.mult).then_inc(xn2_done, 1)
                if k >= 3:
                    dve.wait_ge(x2_hi_done, k - 2)
                    nc.vector.tensor_tensor(x2_lo[:, k - 3, :], XT2, x2_hi[:, k - 3, :].bitcast(F32),
                                            ALU.subtract).then_inc(x2_lo_done, 1)

            for b in range(B):
                dve.wait_ge(gate_ps, b + 1)
                nc.vector.tensor_copy(logit[:, b, :, 0:E], psum[:, GATE_BANKS[b], 0:NT * E].rearrange("p (n e) -> p n e", e=E)).then_inc(logit_done, 1)
                dve.wait_ge(logit_done, b + 1)
                for n in range(NT):
                    nc.vector.max(top8[:, b, n, :], logit[:, b, n, 0:E]).then_inc(top8_done, 1)
                dve.wait_ge(top8_done, (b + 1) * NT)
                nc.vector.tensor_tensor(gd[:, b, :, :], logit[:, b, :, 0:E], top8[:, b, :, 0:1].to_broadcast([P, NT, E]),
                                        ALU.subtract).then_inc(gd_done, 1)
                nc.vector.tensor_copy(best[:, b, :, 0:2], top8[:, b, :, 0:2]).then_inc(best_done, 1)
                dve.wait_ge(best_done, b + 1)
                for n in range(NT):
                    nc.vector.match_replace(found[:, b, n, :], best[:, b, n, :], logit[:, b, n, :], FOUND).then_inc(found_done, 1)
                dve.wait_ge(gexp_done, b + 1)
                nc.vector.tensor_reduce(gsum[:, b, :], gexp[:, b, :, :], AX_X, ALU.add).then_inc(gsum_done, 1)
                dve.wait_ge(found_done, (b + 1) * NT)
                nc.vector.scalar_tensor_tensor(gpick[:, b, :, :], found[:, b, :, 0:E], 0.5 * FOUND, gexp[:, b, :, :],
                                               ALU.is_ge, ALU.mult).then_inc(gpick_done, 1)
                dve.wait_ge(gsum_done, b + 1)
                nc.vector.reciprocal(grec[:, b, :], gsum[:, b, :]).then_inc(grec_done, 1)
                dve.wait_ge(grec_done, b + 1)
                nc.vector.tensor_scalar(gscale[:, b, :], grec[:, b, :], tanh_g[:, 1:2], None, ALU.mult).then_inc(gscale_done, 1)
                dve.wait_ge(gscale_done, b + 1)
                dve.wait_ge(gpick_done, b + 1)
                nc.vector.tensor_tensor(cw[:, b, :, :], gpick[:, b, :, :], gscale[:, b, :].unsqueeze(2).to_broadcast([P, NT, E]),
                                        ALU.mult).then_inc(cw_done, 1)
                dve.wait_ge(cw_done, b + 1)
                nc.vector.tensor_copy(cw_hl[:, b, :, 0:E], cw[:, b, :, :]).then_inc(cw_hi_done, 1)
                dve.wait_ge(cw_hi_done, b + 1)
                nc.vector.tensor_tensor(cw_hl[:, b, :, E:2 * E], cw[:, b, :, :], cw_hl[:, b, :, 0:E].bitcast(F32),
                                        ALU.subtract).then_inc(cw_lo_done, 1)
            for b in range(B):
                dve.wait_ge(cwT_ps, b + 1)
                nc.vector.tensor_copy(cwT[:, b, :], psum[0:2 * E, CWT_BANK, :]).then_inc(cwT_done, 1)

            def weight_y(s, b):
                dve.wait_ge(y_ps, s + 1)
                dve.wait_ge(cwb_done, s + 1)
                if not isinstance(s, int) or s >= B:
                    dve.wait_ge(acc_done, s - 1)
                nc.vector.tensor_tensor(y_cw[:, b, :], psum[:, Y_BANKS[b], :], cwb[:, b, :], ALU.mult).then_inc(y_cw_done, 1)

            def pair(i, first=False):
                for j in range(PT_TILES):
                    g, s, m = PT_TILES * i + j, 2 * B * i + j // MT, j % MT
                    dve.wait_ge(g_hi_done, g + 1)
                    nc.vector.tensor_tensor(g_lo[:, j % 4, :], psum[:, j % 4, :], g_hi[:, j % 4, :].bitcast(F32),
                                            ALU.subtract).then_inc(g_lo_done, 1)
                    if m == LAG - 1 and not (first and j < MT):
                        weight_y(s - 1, (j // MT - 1) % B)

            pair(0, first=True)
            with dve.Fori(1, PAIRS) as i:
                pair(i)
            weight_y(STEPS - 1, 1)
            for b in range(B):
                dve.wait_ge(fin_ps, b + 1)
                nc.vector.tensor_tensor(fin[:, b, :].rearrange("p (n d) -> p n d", n=NT),
                                        psum[:, FIN_BANKS[b], :].rearrange("p (n d) -> p n d", n=NT),
                                        x1[:, b * NT:(b + 1) * NT, :], ALU.add).then_inc(fin_done, 1)

        @block.tensor
        def _(pe):
            def xT1(k):
                pe.wait_ge(xn1_done, k + 1)
                if k >= 1:
                    pe.wait_ge(xT1_lo_done, k)
                nc.tensor.transpose(XT1, xn1[:, k, :], ident[:, :]).then_inc(xT1_ps, 1)

            def three(acc_out, hi, lo, r_hi, r_lo, start=True, stop=True):
                nc.tensor.matmul(acc_out, hi, r_hi, start=start, stop=False)
                nc.tensor.matmul(acc_out, hi, r_lo, start=False, stop=False)
                return nc.tensor.matmul(acc_out, lo, r_hi, start=False, stop=stop)

            def scores(k):
                b = k // NT
                pe.wait_ge(xT1_lo_done, k + 1)
                if k >= 1:
                    pe.wait_ge(ssub_done, k)
                for half in range(2):
                    heads = slice(half * HEADS // 2, (half + 1) * HEADS // 2)
                    last = three(psum[:, half, 0:HH], xnT_hi[k % 2][:, :], xnT_lo[k % 2][:, :],
                                 a_hi[:, b, heads, :].rearrange("p h m -> p (h m)"),
                                 a_lo[:, b, heads, :].rearrange("p h m -> p (h m)"))
                last.then_inc(sc_ps, 1)

            pe.wait_ge(ident_done, 1)
            pe.wait_ge(d_ctx, 16)
            for b in range(B):
                last = nc.tensor.transpose(psum[:, 7, b * M:(b + 1) * M], ctx_sb[:, b, :], ident[0:M, 0:M])
            last.then_inc(ctxT_ps, 1)
            pe.wait_ge(d_wq, 16)
            for j in range(J):
                last = nc.tensor.transpose(psum[:, 6, j * P:(j + 1) * P], wq_sb[:, j * P:(j + 1) * P], ident[:, :])
            last.then_inc(wqT_ps, 1)
            pe.wait_ge(ctxT_done, 1)
            for w_sb, d_w, ps, bank in ((wk_sb, d_wk, kT_ps, 0), (wv_sb, d_wv, vT_ps, 2)):
                pe.wait_ge(d_w, 16)
                for j in range(J):
                    last = nc.tensor.matmul(psum[:, bank + j // 2, (j % 2) * B * M:(j % 2 + 1) * B * M],
                                            w_sb[:, j * P:(j + 1) * P], ctxT[:, :], start=True, stop=True)
                    if j % 2:
                        last.then_inc(ps, 1)
            xT1(0)
            pe.wait_ge(kT_done, 2)
            pe.wait_ge(wqT_done, 1)
            for bank in range(4):
                if bank == 2:
                    pe.wait_ge(v_done, 8)
                parity, half = bank // 2, bank % 2
                rows = slice(parity * HD, (parity + 1) * HD)
                for c in range(2):
                    last = nc.tensor.matmul(psum[:, bank, c * B * M:(c + 1) * B * M], wqT[rows, 2 * half + c, :],
                                            kT[rows, 2 * half + c, :], start=True, stop=True)
                last.then_inc(a_ps, 1)
            pe.wait_ge(d_b1, 16)
            pe.wait_ge(d_wg, 16)
            nc.tensor.transpose(psum[:, 7, 320:320 + E], wg_sb[:, :], ident[0:E, 0:E])
            nc.tensor.transpose(psum[:, 7, 352:352 + E * MT], b1_sb[:, :], ident[0:E * MT, 0:E * MT]).then_inc(small_ps, 1)
            xT1(1)
            pe.wait_ge(a_lo_done, 4)
            scores(0)
            pe.wait_ge(d_wo, 16)
            pe.wait_ge(small_done, 1)
            pe.wait_ge(wg_lo_done, 1)
            for idx in range(B * CH):
                b, c = idx // CH, idx % CH
                js = [j for j in (c - 1, c) if 0 <= j < J]
                for j in js:
                    at = (b * J + j) * BW + (c - j) * P
                    last = nc.tensor.matmul(psum[:, VO_BANKS[idx // 4], (idx % 4) * D:(idx % 4 + 1) * D],
                                            v_blocks[:, at:at + P], wo_sb[:, j, :], start=(j == js[0]), stop=(j == js[-1]))
                if idx % 4 == 3 or idx == B * CH - 1:
                    last.then_inc(vo_ps, 1)

            for k in range(T + 2):
                if 1 <= k <= T:
                    pe.wait_ge(pT_lo_done, k)
                    if k == 1:
                        pe.wait_ge(vo_lo_done, 3)
                    else:
                        pe.wait_ge(x1_done, k - 1)
                    b = (k - 1) // NT
                    for c in range(CH):
                        cols = slice(c * P, (c + 1) * P)
                        last = three(AO, pT_hi[(k - 1) % 2][:, cols], pT_lo[(k - 1) % 2][:, cols],
                                     vo_hi[:, b * CH + c, :], vo_lo[:, b * CH + c, :], start=(c == 0), stop=(c == CH - 1))
                    last.then_inc(ao_ps, 1)
                if k + 1 < T:
                    scores(k + 1)
                if k + 2 < T:
                    xT1(k + 2)
                if k >= 2:
                    pe.wait_ge(xn2_done, k - 1)
                    if k >= 3:
                        pe.wait_ge(x2_lo_done, k - 2)
                    nc.tensor.transpose(XT2, xn2[:, k - 2, :], ident[:, :]).then_inc(xT2_ps, 1)
                if k < T:
                    pe.wait_ge(norm_done, k + 1)
                    if k >= 1:
                        pe.wait_ge(pT_lo_done, k)
                    for c in range(CH):
                        last = nc.tensor.transpose(psum_flat[:, 2 * 512 + c * P:2 * 512 + (c + 1) * P],
                                                   prob[:, k % 2, c * P:(c + 1) * P], ident[:, :])
                    last.then_inc(pT_ps, 1)

            pe.wait_ge(x2_lo_done, T)
            for b in range(B):
                for n in range(NT):
                    t = b * NT + n
                    last = three(psum[:, GATE_BANKS[b], n * E:(n + 1) * E], x2_hi[:, t, :], x2_lo[:, t, :],
                                 wg_hi[:, :], wg_lo[:, :])
                last.then_inc(gate_ps, 1)

            def combine():
                for b in range(B):
                    pe.wait_ge(cw_lo_done, b + 1)
                    if b >= 1:
                        pe.wait_ge(cwT_done, b)
                    for n in range(NT):
                        last = nc.tensor.transpose(psum[0:2 * E, CWT_BANK, n * P:(n + 1) * P],
                                                   cw_hl[:, b, n, :].bitcast(F32), ident[:, :])
                    last.then_inc(cwT_ps, 1)
                pe.wait_ge(b2_lo_done, 1)
                for b in range(B):
                    pe.wait_ge(cwT_done, b + 1)
                    if b >= 1:
                        pe.wait_ge(acc_init, b)
                    nc.tensor.matmul(psum[:, B2_BANK, :], b2_hi[:, :], cwT[:, b, :], start=True, stop=False)
                    nc.tensor.matmul(psum[:, B2_BANK, :], b2_lo[0:E, :], cwT[0:E, b, :], start=False, stop=True).then_inc(b2_ps, 1)

            def second(i, j, first=False):
                u, b, m = j // (B * MT), j // MT % B, j % MT
                pe.wait_ge(g_lo_done, PT_TILES * i + j + 1)
                if m == 0 and not (first and j < B * MT):
                    pe.wait_ge(y_cw_done, 2 * B * i + j // MT - 1)
                elif m == 0:
                    pe.wait_ge(acc_init, B)
                last = three(psum[:, Y_BANKS[b], :], w2_hi[u][:, m, :], w2_lo[u][:, m, :], g_hi[:, j % 4, :], g_lo[:, j % 4, :],
                             start=(m == 0), stop=(m == MT - 1))
                if m == MT - 1:
                    last.then_inc(y_ps, 1)

            def pair(i, first=False):
                for j in range(PT_TILES):
                    u, b, m = j // (B * MT), j // MT % B, j % MT
                    if j % (B * MT) == 0:
                        pe.wait_ge(w_split, 4 * (2 * i + u) + 4)
                    if not (first and j < 4):
                        pe.wait_ge(g_lo_done, PT_TILES * i + j - 3)
                    toks = slice(b * NT, (b + 1) * NT)
                    cols = slice(m * P, (m + 1) * P)
                    three(psum[:, j % 4, :], w1_hi[u][:, cols], w1_lo[u][:, cols],
                          x2_hi[:, toks, :].rearrange("p n t -> p (n t)"),
                          x2_lo[:, toks, :].rearrange("p n t -> p (n t)")).then_inc(h_ps, 1)
                    if first and j == LAG - 1:
                        combine()
                    if m == MT - 1:
                        if not (first and j < B * MT):
                            pe.wait_ge(cwb_done, 2 * B * i + j // MT - 1)
                        nc.tensor.matmul(psum[:, CWB_BANKS[b], :], sel_e[u][:, :], cwT[:, b, :], start=True, stop=True).then_inc(cwb_ps, 1)
                    if j >= LAG:
                        second(i, j - LAG, first)
                    elif not first:
                        second(i - 1, j - LAG + PT_TILES)

            pair(0, first=True)
            with pe.Fori(1, PAIRS) as i:
                pair(i)
            for j in range(PT_TILES - LAG, PT_TILES):
                second(PAIRS - 1, j)
            for b in range(B):
                pe.wait_ge(acc_done, STEPS - 1 + b)
                pe.wait_ge(cwb_done, STEPS - 1 + b)
                for n in range(NT):
                    last = nc.tensor.transpose(psum[:, FIN_BANKS[b], n * P:(n + 1) * P], acc[:, b, n * P:(n + 1) * P], ident[:, :])
                last.then_inc(fin_ps, 1)


INPUTS = ["x", "ctx_1024", "g_xattn", "g_ffn", "L0_xattn_Wq", "L0_xattn_Wk", "L0_xattn_Wv", "L0_xattn_Wo", "L0_xattn_bo",
          "L0_ffn_w_gate", "L0_ffn_W1", "L0_ffn_b1", "L0_ffn_W2", "L0_ffn_b2"]


def kernel(**inputs):
    import numpy as np
    import concourse.bacc as bacc
    from concourse.bass_utils import run_bass_kernel_spmd

    nc = bacc.Bacc("TRN2", target_bir_lowering=False, num_devices=1)
    arrays, args = {}, []
    for name in INPUTS:
        a = np.ascontiguousarray(inputs[name])
        arrays[f"in_{name}"] = a
        args.append(nc.dram_tensor(f"in_{name}", a.shape, mybir.dt.from_np(a.dtype), kind="ExternalInput").ap())
    out = nc.dram_tensor("out_x", arrays["in_x"].shape, F32, kind="ExternalOutput").ap()
    flamingo_block(nc, *args, out)
    return run_bass_kernel_spmd(nc, [arrays], core_ids=[0]).results[0]["out_x"]
```

```python
from contextlib import ExitStack

import concourse.bass as bass
from concourse import mybir

F32 = mybir.dt.float32
F32R = mybir.dt.float32r
ALU = mybir.AluOpType
ACT = mybir.ActivationFunctionType
AX_X = mybir.AxisListType.X

P = 128
HEADS = 8
EPS = 1e-5
JUNK = -3.0e38
FOUND = 3.0e38
EULER = 2.718281828459045


def flamingo_block(nc, x, ctx_in, g_xattn, g_ffn, Wq, Wk, Wv, Wo, bo, w_gate, W1, b1, W2, b2, out):
    B, S, D = x.shape
    M = ctx_in.shape[1]
    INNER = Wq.shape[1]
    HD = INNER // HEADS
    E, _, HID = W1.shape
    assert D == P and HD == 64 and E == 8 and HID % P == 0 and S % P == 0
    NT = S // P
    T = B * NT
    J = INNER // P
    HM = HEADS * M
    HH = HM // 2
    CH = -(-HM // P)
    HMP = CH * P
    MT = HID // P
    STEPS = E * B
    G = STEPS * MT
    LAG = 3
    PAIRS = E // 2
    PT_TILES = 2 * B * MT
    BW = 2 * P
    GT = 2

    with ExitStack() as stack:
        def sb(name, shape, dt=F32):
            return stack.enter_context(nc.sbuf_tensor(name, shape, dt))

        def sem(name):
            return stack.enter_context(nc.semaphore(name))

        psum = stack.enter_context(nc.psum_tensor("psum", [P, 8, 512], F32))
        psum_flat = psum[:, :, :].rearrange("p b n -> p (b n)")

        x_sb = sb("x_sb", [P, B, NT, D])
        ctx_sb = sb("ctx_sb", [M, B, D])
        wq_sb = sb("wq_sb", [P, INNER])
        wk_sb = sb("wk_sb", [P, INNER])
        wv_sb = sb("wv_sb", [P, INNER])
        wo_sb = sb("wo_sb", [P, J, D])
        bo_sb = sb("bo_sb", [P, D])
        gates_in = sb("gates_in", [P, 2])
        wg_sb = sb("wg_sb", [E, D])
        b1_sb = sb("b1_sb", [E * MT, P])
        b2_sb = sb("b2_sb", [2 * E, D])
        w1_sb = sb("w1_sb", [P, E, HID])
        w2_sb = sb("w2_sb", [P, E, MT, D])
        ident = sb("ident", [P, P])
        minus_half = sb("minus_half", [P, T])
        euler = sb("euler", [P, NT, E])
        sel_f = sb("sel_f", [2 * E, E, P])
        tanh_g = sb("tanh_g", [P, 2])
        tbo = sb("tbo", [P, D])
        wqT = sb("wqT", [P, J, D])
        ctxT = sb("ctxT", [P, B * M])
        kT = sb("kT", [P, J, B * M])
        v_blocks = sb("v_blocks", [P, B * J * BW + BW])
        a_hi = sb("a_hi", [P, B, HEADS, M], F32R)
        a_lo = sb("a_lo", [P, B, HEADS, M], F32R)
        vo_hi = sb("vo_hi", [P, B, HMP], F32R)
        vo_lo = sb("vo_lo", [P, B, HMP], F32R)
        wg_hi = sb("wg_hi", [P, E], F32R)
        wg_lo = sb("wg_lo", [P, E], F32R)
        b1T = sb("b1T", [P, E * MT])
        b2_hi = sb("b2_hi", [2 * E, D], F32R)
        b2_lo = sb("b2_lo", [2 * E, D], F32R)
        bn1 = sb("bn1", [P, T, 6])
        mv1 = sb("mv1", [P, T, 2])
        ve1 = sb("ve1", [P, T])
        rstd1 = sb("rstd1", [P, T])
        xb = sb("xb", [P, T, D])
        xn1 = sb("xn1", [P, T, D])
        xnT_hi = sb("xnT_hi", [P, T, P], F32R)
        xnT_lo = sb("xnT_lo", [P, T, P], F32R)
        smax = sb("smax", [P, 2, HEADS])
        ssum = sb("ssum", [P, 2, HEADS])
        srec = sb("srec", [P, 2, HEADS])
        prob = sb("prob", [P, 2, HMP])
        pT_hi = [sb(f"pT_hi{u}", [P, HMP], F32R) for u in range(2)]
        pT_lo = [sb(f"pT_lo{u}", [P, HMP], F32R) for u in range(2)]
        x1 = sb("x1", [P, T, D])
        bn2 = sb("bn2", [P, T, 6])
        mv2 = sb("mv2", [P, T, 2])
        ve2 = sb("ve2", [P, T])
        rstd2 = sb("rstd2", [P, T])
        xn2 = sb("xn2", [P, T, D])
        x2_hi = sb("x2_hi", [P, T, P], F32R)
        x2_lo = sb("x2_lo", [P, T, P], F32R)
        logit = sb("logit", [P, B, NT, E + 6])
        top8 = sb("top8", [P, B, NT, 8])
        best = sb("best", [P, B, NT, 8])
        found = sb("found", [P, B, NT, E + 6])
        gd = sb("gd", [P, B, NT, E])
        gexp = sb("gexp", [P, B, NT, E])
        gsum = sb("gsum", [P, B, NT])
        grec = sb("grec", [P, B, NT])
        gscale = sb("gscale", [P, B, NT])
        gpick = sb("gpick", [P, B, NT, E])
        cw = sb("cw", [P, B, NT, E])
        cw_hl = sb("cw_hl", [P, B, NT, 2 * E], F32R)
        cwT = sb("cwT", [2 * E, B, S], F32R)
        b1_e = [sb(f"b1_e{u}", [P, MT]) for u in range(2)]
        sel_e = [sb(f"sel_e{u}", [2 * E, P], F32R) for u in range(2)]
        cwb = sb("cwb", [P, B, S])
        w1_hi = [sb(f"w1_hi{u}", [P, HID], F32R) for u in range(2)]
        w1_lo = [sb(f"w1_lo{u}", [P, HID], F32R) for u in range(2)]
        w2_hi = [sb(f"w2_hi{u}", [P, MT, D], F32R) for u in range(2)]
        w2_lo = [sb(f"w2_lo{u}", [P, MT, D], F32R) for u in range(2)]
        g_hi = sb("g_hi", [P, 4, S], F32R)
        g_lo = sb("g_lo", [P, 4, S], F32R)
        y_cw = sb("y_cw", [P, 2, S])
        acc = sb("acc", [P, B, S])
        fin = sb("fin", [P, B, NT * D])

        SC = [psum[:, 2 * u:2 * u + 2, 0:HH].rearrange("p b (h m) -> p b h m", m=M) for u in range(2)]
        PT = psum_flat[:, 4 * 512:4 * 512 + HMP]
        VO_PS = [psum_flat[:, bank * 512:bank * 512 + HMP] for bank in (4, 6)]
        AO = psum[:, 6, 0:D]
        X_BANK = 7
        GATE_COL = 384
        SMALL_BANK = 6
        CW_BANKS = (6, 7)
        Y_BANKS, CWB_BANKS = (4, 5), (6, 7)
        FIN_PARTS = ((0, 0, NT), (1, 0, NT // 2), (1, NT // 2, NT))

        def fin_psum(b, n0, n1):
            if b == 0:
                return psum[:, 6, :].rearrange("p (n d) -> p n d", d=D)
            return psum[:, n0:n1, 0:D]

        d_ctx, d_wq, d_wk, d_wv, d_wo = sem("d_ctx"), sem("d_wq"), sem("d_wk"), sem("d_wv"), sem("d_wo")
        d_x = [sem(f"d_x{b}") for b in range(B)]
        d_bo, d_g, d_wg, d_b1, d_b2 = sem("d_bo"), sem("d_g"), sem("d_wg"), sem("d_b1"), sem("d_b2")
        d_w1 = [sem(f"d_w1_{i}") for i in range(2)]
        d_w2 = [sem(f"d_w2_{i}") for i in range(2)]
        d_out = sem("d_out")
        ident_zero, ident_done = sem("ident_zero"), sem("ident_done")
        consts_done, sel_zero, sel_steps, sel_done = sem("consts_done"), sem("sel_zero"), sem("sel_steps"), sem("sel_done")
        vzero_done = sem("vzero_done")
        wqT_ps, wqT_done = sem("wqT_ps"), sem("wqT_done")
        ctxT_ps, ctxT_done = sem("ctxT_ps"), sem("ctxT_done")
        small_ps, small_done = sem("small_ps"), sem("small_done")
        wg_hi_done, wg_lo_done, b2_hi_done, b2_lo_done = sem("wg_hi_done"), sem("wg_lo_done"), sem("b2_hi_done"), sem("b2_lo_done")
        kT_ps, kT_done, vT_ps, v_done = sem("kT_ps"), sem("kT_done"), sem("vT_ps"), sem("v_done")
        a_ps, a_hi_done, a_lo_done = sem("a_ps"), sem("a_hi_done"), sem("a_lo_done")
        vo_ps, vo_hi_done, vo_lo_done = sem("vo_ps"), sem("vo_hi_done"), sem("vo_lo_done")
        tanh_done, tbo_done, xb_done = sem("tanh_done"), sem("tbo_done"), sem("xb_done")
        bn1_done, mv1_done, ve1_done, rstd1_done, xn1_done = sem("bn1_done"), sem("mv1_done"), sem("ve1_done"), sem("rstd1_done"), sem("xn1_done")
        xT1_ps, xT1_hi_done, xT1_lo_done = sem("xT1_ps"), sem("xT1_hi_done"), sem("xT1_lo_done")
        sc_ps, smax_done, exp_done = sem("sc_ps"), sem("smax_done"), sem("exp_done")
        srec_done, norm_done = sem("srec_done"), sem("norm_done")
        pT_ps, pT_hi_done, pT_lo_done = sem("pT_ps"), sem("pT_hi_done"), sem("pT_lo_done")
        ao_ps, x1_done, bn2_done, mv2_done = sem("ao_ps"), sem("x1_done"), sem("bn2_done"), sem("mv2_done")
        ve2_done, rstd2_done, xn2_done = sem("ve2_done"), sem("rstd2_done"), sem("xn2_done")
        xT2_ps, x2_hi_done, x2_lo_done = sem("xT2_ps"), sem("x2_hi_done"), sem("x2_lo_done")
        gate_ps, logit_done, top8_done, best_done = sem("gate_ps"), sem("logit_done"), sem("top8_done"), sem("best_done")
        found_done, gd_done, gsum_done = sem("found_done"), sem("gd_done"), sem("gsum_done")
        gexp0_done, gexp1_done = sem("gexp0_done"), sem("gexp1_done")
        grec_done, gscale_done, gpick_done, cw_done = sem("grec_done"), sem("gscale_done"), sem("gpick_done"), sem("cw_done")
        cw_hi_done, cw_lo_done, cwT_ps, cwT_done = sem("cw_hi_done"), sem("cw_lo_done"), sem("cwT_ps"), sem("cwT_done")
        cwb_ps, cwb_done, b2_ps, acc_init = sem("cwb_ps"), sem("cwb_done"), sem("b2_ps"), sem("acc_init")
        w_hi_done, w_hi_seen, w_split = sem("w_hi_done"), sem("w_hi_seen"), sem("w_split")
        h_ps, gelu_done, g_hi_done, g_lo_done = sem("h_ps"), sem("gelu_done"), sem("g_hi_done"), sem("g_lo_done")
        y_ps, y_cw_done, acc_done = sem("y_ps"), sem("y_cw_done"), sem("acc_done")
        fin_ps, fin_done = sem("fin_ps"), sem("fin_done")

        A_BANKS = (0, 1, 4, 5)

        def a_psum(bank):
            return psum[:, A_BANKS[bank], 0:2 * B * M].rearrange("p (c b m) -> p b c m", c=2, b=B)

        def a_view(t, bank):
            first = 4 * (bank % 2) + bank // 2
            return t[:, :, first:first + 3:2, :]

        block = stack.enter_context(nc.Block())

        def place(j, first):
            step = j // MT
            return (step % B, step // B) if first else (step // B, step % B)

        CWB_AT = (6, 8, 14, 15)

        @block.sync
        def _(sp):
            sp.dma_start(ctx_sb[:, :, :], ctx_in.rearrange("b m d -> m b d")).then_inc(d_ctx, 16)
            sp.dma_start(wk_sb[:, :], Wk).then_inc(d_wk, 16)
            sp.dma_start(x_sb[:, 0, :, :], x[0].rearrange("(p n) d -> p n d", n=NT)).then_inc(d_x[0], 16)
            sp.dma_start(wo_sb[:, :, :], Wo.rearrange("(j p) d -> p j d", p=P)).then_inc(d_wo, 16)
            sp.dma_start(x_sb[:, 1, :, :], x[1].rearrange("(p n) d -> p n d", n=NT)).then_inc(d_x[1], 16)
            sp.dma_start(wg_sb[:, :], w_gate).then_inc(d_wg, 16)
            sp.dma_start(b1_sb[:, :], b1.rearrange("e (m p) -> (e m) p", p=P)).then_inc(d_b1, 16)
            for half in range(2):
                sp.dma_start(b2_sb[half * E:(half + 1) * E, :], b2).then_inc(d_b2, 16)
            for i in range(2):
                half = slice(i * E // 2, (i + 1) * E // 2)
                sp.dma_start(w1_sb[:, half, :], W1[half].rearrange("e d h -> d e h")).then_inc(d_w1[i], 16)
                for e in range(i * E // 2, (i + 1) * E // 2):
                    sp.dma_start(w2_sb[:, e, :, :], W2[e].rearrange("(k p) d -> p k d", p=P)).then_inc(d_w2[i], 16)
            for f, (b, n0, n1) in enumerate(FIN_PARTS):
                sp.wait_ge(fin_done, f + 1)
                cols = slice(n0 * D, n1 * D)
                sp.dma_start(out[b].rearrange("(p n) d -> p (n d)", n=NT)[:, cols], fin[:, b, cols]).then_inc(d_out, 16)
            sp.wait_ge(d_out, 16 * len(FIN_PARTS))

        @block.gpsimd
        def _(pool):
            nc.gpsimd.memset(ident[:, :], 0.0).then_inc(ident_zero, 1)
            pool.wait_ge(ident_zero, 1)
            nc.gpsimd.affine_select(out=ident[:, :], in_=ident[:, :], compare_op=ALU.not_equal, fill=1.0, base=0,
                                    pattern=[[-1, P]], channel_multiplier=1).then_inc(ident_done, 1)
            nc.gpsimd.memset(minus_half[:, :], -0.5).then_inc(consts_done, 1)
            nc.gpsimd.memset(v_blocks[:, :], 0.0).then_inc(vzero_done, 1)
            nc.gpsimd.memset(euler[:, :, :], EULER).then_inc(consts_done, 1)
            nc.gpsimd.memset(prob[:, :, HM:HMP], 0.0).then_inc(consts_done, 1)
            nc.gpsimd.memset(logit[:, :, :, E:E + 6], JUNK).then_inc(consts_done, 1)
            nc.gpsimd.memset(best[:, :, :, 2:8], JUNK).then_inc(consts_done, 1)
            def rstd1_of(b):
                tiles = slice(b * NT, (b + 1) * NT)
                pool.wait_ge(mv1_done, (b + 1) * NT)
                nc.gpsimd.tensor_scalar(ve1[:, tiles], mv1[:, tiles, 1], EPS, None, ALU.add).then_inc(ve1_done, 1)
                pool.wait_ge(ve1_done, b + 1)
                if b == 0:
                    pool.wait_ge(consts_done, 5)
                nc.gpsimd.tensor_tensor(rstd1[:, tiles], ve1[:, tiles], minus_half[:, tiles], ALU.pow).then_inc(rstd1_done, 1)

            rstd1_of(0)
            nc.gpsimd.memset(sel_f[:, :, :], 0.0).then_inc(sel_zero, 1)
            pool.wait_ge(d_bo, 16)
            pool.wait_ge(tanh_done, 1)
            nc.gpsimd.tensor_scalar(tbo[:, :], bo_sb[:, :], tanh_g[:, 0:1], None, ALU.mult).then_inc(tbo_done, 1)
            pool.wait_ge(tbo_done, 1)
            for b in range(B):
                pool.wait_ge(d_x[b], 16)
                nc.gpsimd.tensor_tensor(xb[:, b * NT:(b + 1) * NT, :], x_sb[:, b, :, :],
                                        tbo[:, :].unsqueeze(1).to_broadcast([P, NT, D]), ALU.add).then_inc(xb_done, 1)
            rstd1_of(1)

            def w1_rest(e, u):
                pool.wait_ge(w_hi_done, 2 * e + 1)
                pool.sem_inc(w_hi_seen, 1)
                nc.gpsimd.tensor_tensor(w1_lo[u][:, :], w1_sb[:, e, :], w1_hi[u][:, :].bitcast(F32), ALU.subtract).then_inc(w_split, 1)
                nc.gpsimd.tensor_copy(b1_e[u][:, :], b1T[:, bass.ds(e * MT, MT)]).then_inc(w_split, 1)

            def w2_rest(e, u):
                pool.wait_ge(w_hi_done, 2 * e + 2)
                pool.sem_inc(w_hi_seen, 1)
                nc.gpsimd.tensor_tensor(w2_lo[u][:, :, :], w2_sb[:, e, :, :], w2_hi[u][:, :, :].bitcast(F32), ALU.subtract).then_inc(w_split, 1)

            def one_hot(e, u):
                nc.gpsimd.tensor_copy(sel_e[u][:, :], sel_f[:, e, :]).then_inc(w_split, 1)

            def split_lo(e, u):
                w1_rest(e, u)
                w2_rest(e, u)
                one_hot(e, u)

            def rstd2_of(q):
                tiles = slice(q * GT, (q + 1) * GT)
                pool.wait_ge(mv2_done, (q + 1) * GT)
                nc.gpsimd.tensor_scalar(ve2[:, tiles], mv2[:, tiles, 1], EPS, None, ALU.add).then_inc(ve2_done, 1)
                pool.wait_ge(ve2_done, q + 1)
                nc.gpsimd.tensor_tensor(rstd2[:, tiles], ve2[:, tiles], minus_half[:, tiles], ALU.pow).then_inc(rstd2_done, 1)

            for k in range(T):
                pool.wait_ge(srec_done, k + 1)
                p_k = prob[:, k % 2, 0:HM].rearrange("p (h m) -> p h m", m=M)
                nc.gpsimd.tensor_tensor(p_k, p_k, srec[:, k % 2, :].unsqueeze(2).to_broadcast([P, HEADS, M]),
                                        ALU.mult).then_inc(norm_done, 1)
                if k in (1, 2):
                    pool.wait_ge(sel_zero, 1)
                    half = k - 1
                    nc.gpsimd.affine_select(out=sel_f[:, :, :], in_=sel_f[:, :, :], compare_op=ALU.not_equal, fill=1.0,
                                            base=-half * E, pattern=[[-1, E], [0, P]], channel_multiplier=1).then_inc(sel_steps, 1)
                    pool.wait_ge(sel_steps, half + 1)
                if k >= 4 and k % 2 == 0:
                    rstd2_of((k - 4) // 2)
                if k == 3:
                    pool.wait_ge(small_done, 1)
                    w1_rest(0, 0)
                if k == 4:
                    w2_rest(0, 0)
                if k == 5:
                    one_hot(0, 0)
                if k == 6:
                    w1_rest(1, 1)
                if k == 7:
                    w2_rest(1, 1)
            rstd2_of(2)
            one_hot(1, 1)
            rstd2_of(3)
            pool.wait_ge(gd_done, B)
            nc.gpsimd.tensor_tensor(gexp[:, 1, :, :], euler[:, :, :], gd[:, 1, :, :], ALU.pow).then_inc(gexp1_done, 1)

            def add_y(s, r, b):
                pool.wait_ge(y_cw_done, s + 1)
                if isinstance(s, int) and s in (0, B):
                    pool.wait_ge(acc_init, s // B + 1)
                else:
                    pool.wait_ge(acc_done, s)
                nc.gpsimd.tensor_tensor(acc[:, b, :], acc[:, b, :], y_cw[:, r, :], ALU.add).then_inc(acc_done, 1)

            def expert(e, u, last=False):
                if not last:
                    split_lo(e + 1, 1 - u)
                add_y(B * e - 1, 1, 1)
                add_y(B * e, 0, 0)

            add_y(0, 0, 0)
            add_y(1, 1, 0)
            pool.wait_ge(gelu_done, 3 * MT)
            w1_rest(2, 0)
            add_y(2, 0, 1)
            w2_rest(2, 0)
            pool.wait_ge(cwb_ps, 3)
            one_hot(2, 0)
            with pool.Fori(1, PAIRS - 1) as i:
                expert(2 * i, 0)
                expert(2 * i + 1, 1)
            expert(E - 2, 0)
            expert(E - 1, 1, last=True)

        @block.scalar
        def _(act):
            act.dma_start(gates_in[:, 0:1], g_xattn.partition_broadcast(P)).then_inc(d_g, 16)
            act.dma_start(gates_in[:, 1:2], g_ffn.partition_broadcast(P)).then_inc(d_g, 16)
            act.dma_start(wq_sb[:, :], Wq).then_inc(d_wq, 16)
            act.dma_start(wv_sb[:, :], Wv).then_inc(d_wv, 16)
            act.dma_start(bo_sb[:, :], bo.partition_broadcast(P)).then_inc(d_bo, 16)
            act.wait_ge(d_g, 32)
            nc.scalar.activation(tanh_g[:, :], gates_in[:, :], ACT.Tanh).then_inc(tanh_done, 1)
            for q in range(2):
                act.wait_ge(kT_ps, q + 1)
                nc.scalar.activation(kT[:, 2 * q:2 * q + 2, :], psum[:, q, 0:2 * B * M].rearrange("p (c n) -> p c n", c=2),
                                     ACT.Copy, scale=HD ** -0.5).then_inc(kT_done, 1)
            for bank in range(4):
                act.wait_ge(a_ps, bank + 1)
                nc.scalar.copy(a_view(a_hi, bank), a_psum(bank)).then_inc(a_hi_done, 1)
            def xT1_hi(b):
                act.wait_ge(xT1_ps, b + 1)
                nc.scalar.copy(xnT_hi[:, b * NT:(b + 1) * NT, :], psum[:, X_BANK, :].rearrange("p (n t) -> p n t", n=NT)).then_inc(xT1_hi_done, 1)

            def x2_high(q):
                act.wait_ge(xT2_ps, q + 1)
                nc.scalar.copy(x2_hi[:, q * GT:(q + 1) * GT, :], psum[:, X_BANK, 0:GT * P].rearrange("p (n t) -> p n t", n=GT)).then_inc(x2_hi_done, 1)

            xT1_hi(0)
            act.wait_ge(vzero_done, 1)
            act.wait_ge(vT_ps, 2)
            for b in range(B):
                for par in range(2):
                    rows = slice(par * HD, (par + 1) * HD)
                    at = b * J * BW + par * M
                    stride = BW + 2 * M - P
                    dst = v_blocks[rows, at:at + J * stride].rearrange("p (j c) -> p j c", c=stride)[:, :, 0:M]
                    for half in range(2):
                        src = psum[rows, 2 + half, 0:2 * B * M].rearrange("p (c b m) -> p c b m", c=2, b=B)
                        nc.scalar.copy(dst[:, 2 * half:2 * half + 2, :], src[:, :, b, :]).then_inc(v_done, 1)
            act.wait_ge(small_ps, 1)
            nc.scalar.copy(wg_hi[:, :], psum[:, SMALL_BANK, 320:320 + E]).then_inc(wg_hi_done, 1)
            nc.scalar.copy(b1T[:, :], psum[:, SMALL_BANK, 352:352 + E * MT]).then_inc(small_done, 1)

            act.wait_ge(d_b2, 32)
            nc.scalar.copy(b2_hi[:, :], b2_sb[:, :]).then_inc(b2_hi_done, 1)

            for k in range(T + 1):
                if k < T:
                    act.wait_ge(smax_done, k + 1)
                    if k >= 2:
                        act.wait_ge(pT_ps, k - 1)
                    else:
                        act.wait_ge(consts_done, 5)
                    for h in range(HEADS):
                        nc.scalar.activation(prob[:, k % 2, h * M:(h + 1) * M], SC[k % 2][:, h // 4, h % 4, :], ACT.Exp,
                                             bias=smax[:, k % 2, h:h + 1], accum_out=ssum[:, k % 2, h:h + 1]).then_inc(exp_done, 1)
                if k >= 1:
                    act.wait_ge(pT_ps, k)
                    if k >= 3:
                        act.wait_ge(ao_ps, k - 2)
                    nc.scalar.copy(pT_hi[(k - 1) % 2][:, :], PT).then_inc(pT_hi_done, 1)
                if k < B:
                    act.wait_ge(vo_ps, k + 1)
                    nc.scalar.copy(vo_hi[:, k, :], VO_PS[k]).then_inc(vo_hi_done, 1)
                if k == 2:
                    xT1_hi(1)
                if k in (6, 7):
                    x2_high(k - 6)
            act.wait_ge(gd_done, 1)
            nc.scalar.activation(gexp[:, 0, :, :], gd[:, 0, :, :], ACT.Exp).then_inc(gexp0_done, 1)

            def start_acc(b):
                act.wait_ge(b2_ps, b + 1)
                nc.scalar.copy(acc[:, b, :], psum[:, CW_BANKS[b], :]).then_inc(acc_init, 1)

            def copy_cwb(s, r):
                act.wait_ge(cwb_ps, s + 1)
                if not isinstance(s, int) or s >= B:
                    act.wait_ge(y_cw_done, s - 1)
                nc.scalar.copy(cwb[:, r, :], psum[:, CWB_BANKS[r], :]).then_inc(cwb_done, 1)

            def pair(i, first=False):
                for j in range(PT_TILES):
                    g, s, m = PT_TILES * i + j, 2 * B * i + j // MT, j % MT
                    u, b = place(j, first)
                    act.wait_ge(h_ps, g + 1)
                    nc.scalar.activation(psum[:, j % 4, :], psum[:, j % 4, :], ACT.Gelu,
                                         bias=b1_e[u][:, m:m + 1]).then_inc(gelu_done, 1)
                    if not (first and j == 0):
                        act.wait_ge(gelu_done, g)
                        nc.scalar.copy(g_hi[:, (j - 1) % 4, :], psum[:, (j - 1) % 4, :]).then_inc(g_hi_done, 1)
                    if first and j in (1, 3):
                        x2_high(2 + j // 2)
                    if first and j in (4, 12):
                        start_acc(j // (B * MT))
                    if first and j in CWB_AT:
                        copy_cwb(CWB_AT.index(j), CWB_AT.index(j) % B)
                    elif not first and m == MT - 1:
                        copy_cwb(s, b)

            pair(0, first=True)
            with act.Fori(1, PAIRS) as i:
                pair(i)
            act.wait_ge(gelu_done, G)
            nc.scalar.copy(g_hi[:, 3, :], psum[:, 3, :]).then_inc(g_hi_done, 1)

        @block.vector
        def _(dve):
            def stats1(b):
                dve.wait_ge(d_x[b], 16)
                for t in range(b * NT, (b + 1) * NT):
                    nc.vector.bn_stats(bn1[:, t, :], x_sb[:, b, t % NT, :]).then_inc(bn1_done, 1)
                for t in range(b * NT, (b + 1) * NT):
                    dve.wait_ge(bn1_done, t + 1)
                    nc.vector.bn_aggr(mv1[:, t, :], bn1[:, t, :]).then_inc(mv1_done, 1)

            def normalise1(b):
                dve.wait_ge(rstd1_done, b + 1)
                for t in range(b * NT, (b + 1) * NT):
                    nc.vector.tensor_scalar(xn1[:, t, :], x_sb[:, b, t % NT, :], mv1[:, t, 0:1], rstd1[:, t:t + 1],
                                            ALU.subtract, ALU.mult).then_inc(xn1_done, 1)

            def xT1_lo(b):
                tiles = slice(b * NT, (b + 1) * NT)
                dve.wait_ge(xT1_hi_done, b + 1)
                nc.vector.tensor_tensor(xnT_lo[:, tiles, :], psum[:, X_BANK, :].rearrange("p (n t) -> p n t", n=NT),
                                        xnT_hi[:, tiles, :].bitcast(F32), ALU.subtract).then_inc(xT1_lo_done, 1)

            def row_max(k):
                dve.wait_ge(sc_ps, k + 1)
                nc.vector.tensor_reduce(smax[:, k % 2, :].rearrange("p (b h) -> p b h", b=2), SC[k % 2], AX_X, ALU.max,
                                        negate=True).then_inc(smax_done, 1)

            def x1_tile(t):
                dve.wait_ge(ao_ps, t + 1)
                dve.wait_ge(xb_done, t // NT + 1)
                nc.vector.scalar_tensor_tensor(x1[:, t, :], AO, tanh_g[:, 0:1], xb[:, t, :],
                                               ALU.mult, ALU.add).then_inc(x1_done, 1)

            def stats2(t):
                dve.wait_ge(x1_done, t + 1)
                nc.vector.bn_stats(bn2[:, t, :], x1[:, t, :]).then_inc(bn2_done, 1)
                dve.wait_ge(bn2_done, t + 1)
                nc.vector.bn_aggr(mv2[:, t, :], bn2[:, t, :]).then_inc(mv2_done, 1)

            def normalise2(q):
                dve.wait_ge(rstd2_done, q + 1)
                for t in range(q * GT, (q + 1) * GT):
                    nc.vector.tensor_scalar(xn2[:, t, :], x1[:, t, :], mv2[:, t, 0:1], rstd2[:, t:t + 1],
                                            ALU.subtract, ALU.mult).then_inc(xn2_done, 1)

            def x2_rest(q):
                tiles = slice(q * GT, (q + 1) * GT)
                dve.wait_ge(x2_hi_done, q + 1)
                nc.vector.tensor_tensor(x2_lo[:, tiles, :], psum[:, X_BANK, 0:GT * P].rearrange("p (n t) -> p n t", n=GT),
                                        x2_hi[:, tiles, :].bitcast(F32), ALU.subtract).then_inc(x2_lo_done, 1)

            def split_hi(e, u):
                nc.vector.tensor_copy(w1_hi[u][:, :], w1_sb[:, e, :]).then_inc(w_hi_done, 1)
                nc.vector.tensor_copy(w2_hi[u][:, :, :], w2_sb[:, e, :, :]).then_inc(w_hi_done, 1)

            dve.wait_ge(ctxT_ps, 1)
            nc.vector.tensor_copy(ctxT[:, :], psum[:, 7, 0:B * M]).then_inc(ctxT_done, 1)
            stats1(0)
            dve.wait_ge(wqT_ps, 1)
            nc.vector.tensor_copy(wqT[:, :, :], psum[:, 6, 0:J * D].rearrange("p (j d) -> p j d", j=J)).then_inc(wqT_done, 1)
            normalise1(0)
            for bank in range(4):
                dve.wait_ge(a_hi_done, bank + 1)
                nc.vector.tensor_tensor(a_view(a_lo, bank), a_psum(bank), a_view(a_hi, bank).bitcast(F32),
                                        ALU.subtract).then_inc(a_lo_done, 1)
            xT1_lo(0)
            stats1(1)
            row_max(0)

            for k in range(T + 1):
                if k >= 3:
                    x1_tile(k - 3)
                if k + 1 < T:
                    row_max(k + 1)
                if k < T:
                    dve.wait_ge(exp_done, HEADS * (k + 1))
                    nc.vector.reciprocal(srec[:, k % 2, :], ssum[:, k % 2, :]).then_inc(srec_done, 1)
                if k >= 3:
                    stats2(k - 3)
                if k in (5, 7):
                    normalise2((k - 5) // 2)
                if k >= 1:
                    dve.wait_ge(pT_hi_done, k)
                    nc.vector.tensor_tensor(pT_lo[(k - 1) % 2][:, :], PT, pT_hi[(k - 1) % 2][:, :].bitcast(F32),
                                            ALU.subtract).then_inc(pT_lo_done, 1)
                if k == 0:
                    dve.wait_ge(wg_hi_done, 1)
                    dve.wait_ge(small_done, 1)
                    nc.vector.tensor_tensor(wg_lo[:, :], psum[:, SMALL_BANK, 320:320 + E], wg_hi[:, :].bitcast(F32), ALU.subtract).then_inc(wg_lo_done, 1)
                    dve.wait_ge(b2_hi_done, 1)
                    nc.vector.tensor_tensor(b2_lo[:, :], b2_sb[:, :], b2_hi[:, :].bitcast(F32), ALU.subtract).then_inc(b2_lo_done, 1)
                    normalise1(1)
                if k < B:
                    dve.wait_ge(vo_hi_done, k + 1)
                    nc.vector.tensor_tensor(vo_lo[:, k, :], VO_PS[k], vo_hi[:, k, :].bitcast(F32), ALU.subtract).then_inc(vo_lo_done, 1)
                if k == 2:
                    xT1_lo(1)
                    dve.wait_ge(d_w1[0], 16)
                    dve.wait_ge(d_w2[0], 16 * (E // 2))
                    split_hi(0, 0)
                if k == 4:
                    split_hi(1, 1)
                if k in (6, 7):
                    x2_rest(k - 6)

            def choose(b):
                dve.wait_ge(gate_ps, b + 1)
                nc.vector.tensor_copy(logit[:, b, :, 0:E], psum[:, X_BANK, GATE_COL:GATE_COL + NT * E].rearrange("p (n e) -> p n e", e=E)).then_inc(logit_done, 1)
                dve.wait_ge(logit_done, b + 1)
                for n in range(NT):
                    nc.vector.max(top8[:, b, n, :], logit[:, b, n, 0:E]).then_inc(top8_done, 1)
                dve.wait_ge(top8_done, (b + 1) * NT)
                nc.vector.tensor_tensor(gd[:, b, :, :], logit[:, b, :, 0:E], top8[:, b, :, 0:1].to_broadcast([P, NT, E]),
                                        ALU.subtract).then_inc(gd_done, 1)
                nc.vector.tensor_copy(best[:, b, :, 0:2], top8[:, b, :, 0:2]).then_inc(best_done, 1)
                dve.wait_ge(best_done, b + 1)
                for n in range(NT):
                    nc.vector.match_replace(found[:, b, n, :], best[:, b, n, :], logit[:, b, n, :], FOUND).then_inc(found_done, 1)

            def combine_weights(b):
                dve.wait_ge((gexp0_done, gexp1_done)[b], 1)
                nc.vector.tensor_reduce(gsum[:, b, :], gexp[:, b, :, :], AX_X, ALU.add).then_inc(gsum_done, 1)
                dve.wait_ge(found_done, (b + 1) * NT)
                nc.vector.scalar_tensor_tensor(gpick[:, b, :, :], found[:, b, :, 0:E], 0.5 * FOUND, gexp[:, b, :, :],
                                               ALU.is_ge, ALU.mult).then_inc(gpick_done, 1)
                dve.wait_ge(gsum_done, b + 1)
                nc.vector.reciprocal(grec[:, b, :], gsum[:, b, :]).then_inc(grec_done, 1)
                dve.wait_ge(grec_done, b + 1)
                nc.vector.tensor_scalar(gscale[:, b, :], grec[:, b, :], tanh_g[:, 1:2], None, ALU.mult).then_inc(gscale_done, 1)
                dve.wait_ge(gscale_done, b + 1)
                dve.wait_ge(gpick_done, b + 1)
                nc.vector.tensor_tensor(cw[:, b, :, :], gpick[:, b, :, :], gscale[:, b, :].unsqueeze(2).to_broadcast([P, NT, E]),
                                        ALU.mult).then_inc(cw_done, 1)
                dve.wait_ge(cw_done, b + 1)
                nc.vector.tensor_copy(cw_hl[:, b, :, 0:E], cw[:, b, :, :]).then_inc(cw_hi_done, 1)
                dve.wait_ge(cw_hi_done, b + 1)
                nc.vector.tensor_tensor(cw_hl[:, b, :, E:2 * E], cw[:, b, :, :], cw_hl[:, b, :, 0:E].bitcast(F32),
                                        ALU.subtract).then_inc(cw_lo_done, 1)

            def copy_cwT(b):
                dve.wait_ge(cwT_ps, b + 1)
                nc.vector.tensor_copy(cwT[:, b, :], psum[0:2 * E, CW_BANKS[b], :]).then_inc(cwT_done, 1)

            x1_tile(T - 2)
            stats2(T - 2)
            choose(0)
            normalise2(2)
            combine_weights(0)
            x1_tile(T - 1)
            stats2(T - 1)

            def weight_y(s, r):
                dve.wait_ge(y_ps, s + 1)
                dve.wait_ge(cwb_done, s + 1)
                if not isinstance(s, int) or s >= B:
                    dve.wait_ge(acc_done, s - 1)
                nc.vector.tensor_tensor(y_cw[:, r, :], psum[:, Y_BANKS[r], :], cwb[:, r, :], ALU.mult).then_inc(y_cw_done, 1)

            def pair(i, first=False, last=False):
                for j in range(PT_TILES):
                    g, s, u, m = PT_TILES * i + j, 2 * B * i + j // MT, j // (B * MT), j % MT
                    dve.wait_ge(g_hi_done, g + 1)
                    nc.vector.tensor_tensor(g_lo[:, j % 4, :], psum[:, j % 4, :], g_hi[:, j % 4, :].bitcast(F32),
                                            ALU.subtract).then_inc(g_lo_done, 1)
                    if first:
                        if j == 0:
                            x2_rest(2)
                            normalise2(3)
                        if j == 1:
                            copy_cwT(0)
                        if j == 2:
                            x2_rest(3)
                        if j == 3:
                            choose(1)
                        if j == 7:
                            combine_weights(1)
                        if j == 8:
                            weight_y(0, 0)
                        if j == 11:
                            weight_y(1, 1)
                        if j == 14:
                            weight_y(2, 0)
                        if j == 9:
                            copy_cwT(1)
                        if j == 12:
                            dve.wait_ge(h_ps, 3 * MT)
                            nc.vector.tensor_copy(w1_hi[0][:, :], w1_sb[:, 2, :]).then_inc(w_hi_done, 1)
                        if j == 14:
                            nc.vector.tensor_copy(w2_hi[0][:, :, :], w2_sb[:, 2, :, :]).then_inc(w_hi_done, 1)
                        continue
                    if m == LAG - 1:
                        weight_y(s - 1, (j // MT - 1) % B)
                    if j % (B * MT) == LAG - 1 and not (last and u == 1):
                        split_hi(2 * i + u + 1, 1 - u)

            dve.wait_ge(d_w1[1], 16)
            dve.wait_ge(d_w2[1], 16 * (E // 2))
            pair(0, first=True)
            with dve.Fori(1, PAIRS - 1) as i:
                pair(i)
            pair(PAIRS - 1, last=True)

            def finish(f):
                b, n0, n1 = FIN_PARTS[f]
                dve.wait_ge(fin_ps, f + 1)
                nc.vector.tensor_tensor(fin[:, b, n0 * D:n1 * D].rearrange("p (n d) -> p n d", n=n1 - n0),
                                        fin_psum(b, n0, n1),
                                        x1[:, b * NT + n0:b * NT + n1, :], ALU.add).then_inc(fin_done, 1)

            dve.wait_ge(y_ps, STEPS)
            dve.wait_ge(cwb_done, STEPS)
            dve.wait_ge(acc_done, STEPS - 2)
            for half in range(2):
                toks = slice(half * S // 2, (half + 1) * S // 2)
                nc.vector.tensor_tensor(y_cw[:, 1, toks], psum[:, Y_BANKS[1], toks], cwb[:, 1, toks], ALU.mult).then_inc(y_cw_done, 1)
                if half == 0:
                    finish(0)
            finish(1)
            finish(2)

        @block.tensor
        def _(pe):
            def xT1(b):
                pe.wait_ge(xn1_done, (b + 1) * NT)
                for n in range(NT):
                    last = nc.tensor.transpose(psum[:, X_BANK, n * P:(n + 1) * P], xn1[:, b * NT + n, :], ident[:, :])
                last.then_inc(xT1_ps, 1)

            def three(acc_out, hi, lo, r_hi, r_lo, start=True, stop=True):
                nc.tensor.matmul(acc_out, hi, r_hi, start=start, stop=False)
                nc.tensor.matmul(acc_out, hi, r_lo, start=False, stop=False)
                return nc.tensor.matmul(acc_out, lo, r_hi, start=False, stop=stop)

            def scores(k):
                b = k // NT
                pe.wait_ge(xT1_lo_done, b + 1)
                if k == 1:
                    pe.wait_ge(v_done, 8)
                if k >= 2:
                    pe.wait_ge(exp_done, HEADS * (k - 1))
                for half in range(2):
                    heads = slice(half * HEADS // 2, (half + 1) * HEADS // 2)
                    last = three(psum[:, 2 * (k % 2) + half, 0:HH], xnT_hi[:, k, :], xnT_lo[:, k, :],
                                 a_hi[:, b, heads, :].rearrange("p h m -> p (h m)"),
                                 a_lo[:, b, heads, :].rearrange("p h m -> p (h m)"))
                last.then_inc(sc_ps, 1)

            pe.wait_ge(ident_done, 1)
            pe.wait_ge(d_ctx, 16)
            for b in range(B):
                last = nc.tensor.transpose(psum[:, 7, b * M:(b + 1) * M], ctx_sb[:, b, :], ident[0:M, 0:M])
            last.then_inc(ctxT_ps, 1)

            def project_ctx(w_sb, d_w, ps, bank):
                pe.wait_ge(d_w, 16)
                for j in range(J):
                    last = nc.tensor.matmul(psum[:, bank + j // 2, (j % 2) * B * M:(j % 2 + 1) * B * M],
                                            w_sb[:, j * P:(j + 1) * P], ctxT[:, :], start=True, stop=True)
                    if j % 2:
                        last.then_inc(ps, 1)

            pe.wait_ge(ctxT_done, 1)
            project_ctx(wk_sb, d_wk, kT_ps, 0)
            pe.wait_ge(d_wq, 16)
            for j in range(J):
                last = nc.tensor.transpose(psum[:, 6, j * P:(j + 1) * P], wq_sb[:, j * P:(j + 1) * P], ident[:, :])
            last.then_inc(wqT_ps, 1)
            project_ctx(wv_sb, d_wv, vT_ps, 2)
            pe.wait_ge(kT_done, 2)
            pe.wait_ge(wqT_done, 1)
            for bank in range(4):
                parity, half = bank // 2, bank % 2
                rows = slice(parity * HD, (parity + 1) * HD)
                for c in range(2):
                    last = nc.tensor.matmul(psum[:, A_BANKS[bank], c * B * M:(c + 1) * B * M], wqT[rows, 2 * half + c, :],
                                            kT[rows, 2 * half + c, :], start=True, stop=True)
                last.then_inc(a_ps, 1)
            xT1(0)
            pe.wait_ge(d_b1, 16)
            pe.wait_ge(d_wg, 16)
            nc.tensor.transpose(psum[:, SMALL_BANK, 320:320 + E], wg_sb[:, :], ident[0:E, 0:E])
            nc.tensor.transpose(psum[:, SMALL_BANK, 352:352 + E * MT], b1_sb[:, :], ident[0:E * MT, 0:E * MT]).then_inc(small_ps, 1)
            pe.wait_ge(a_lo_done, 4)
            scores(0)

            def fold_vo(b):
                for c in range(CH):
                    js = [j for j in (c - 1, c) if 0 <= j < J]
                    for j in js:
                        at = (b * J + j) * BW + (c - j) * P
                        last = nc.tensor.matmul(VO_PS[b][:, c * P:(c + 1) * P], v_blocks[:, at:at + P], wo_sb[:, j, :],
                                                start=(j == js[0]), stop=(j == js[-1]))
                last.then_inc(vo_ps, 1)

            def transpose_probs(k):
                pe.wait_ge(norm_done, k + 1)
                if k >= 1:
                    pe.wait_ge(pT_lo_done, k)
                for c in range(CH):
                    cols = slice(c * P, (c + 1) * P)
                    last = nc.tensor.transpose(PT[:, cols], prob[:, k % 2, cols], ident[:, :])
                last.then_inc(pT_ps, 1)

            def attention_out(k):
                pe.wait_ge(pT_lo_done, k + 1)
                if k >= 1:
                    pe.wait_ge(x1_done, k)
                for c in range(CH):
                    cols = slice(c * P, (c + 1) * P)
                    last = three(AO, pT_hi[k % 2][:, cols], pT_lo[k % 2][:, cols], vo_hi[:, k // NT, cols], vo_lo[:, k // NT, cols],
                                 start=(c == 0), stop=(c == CH - 1))
                last.then_inc(ao_ps, 1)

            def xT2(q):
                pe.wait_ge(xn2_done, (q + 1) * GT)
                if q >= 1:
                    pe.wait_ge(x2_lo_done, q)
                if q >= 2:
                    pe.wait_ge(logit_done, 1)
                for n in range(GT):
                    last = nc.tensor.transpose(psum[:, X_BANK, n * P:(n + 1) * P], xn2[:, q * GT + n, :], ident[:, :])
                last.then_inc(xT2_ps, 1)

            def gate_logits(b):
                pe.wait_ge(x2_lo_done, (b + 1) * NT // GT)
                for n in range(NT):
                    t = b * NT + n
                    last = three(psum[:, X_BANK, GATE_COL + n * E:GATE_COL + (n + 1) * E], x2_hi[:, t, :], x2_lo[:, t, :],
                                 wg_hi[:, :], wg_lo[:, :])
                last.then_inc(gate_ps, 1)

            for k in range(T + 1):
                if k + 1 < T:
                    scores(k + 1)
                if k == 0:
                    pe.wait_ge(d_wo, 16)
                    fold_vo(0)
                if k >= 1:
                    if k == 1:
                        pe.wait_ge(vo_lo_done, 1)
                    transpose_probs(k - 1)
                if k == 1:
                    pe.wait_ge(small_done, 1)
                    pe.wait_ge(wg_lo_done, 1)
                    fold_vo(1)
                if k == 2:
                    pe.wait_ge(vo_lo_done, 2)
                    xT1(1)
                if k >= 2:
                    attention_out(k - 2)
                if k == T:
                    gate_logits(0)
                if k in (5, 7):
                    xT2((k - 5) // 2)

            def transpose_cw(b):
                pe.wait_ge(cw_lo_done, b + 1)
                if b == 0:
                    pe.wait_ge(x1_done, T)
                for n in range(NT):
                    last = nc.tensor.transpose(psum[0:2 * E, CW_BANKS[b], n * P:(n + 1) * P],
                                               cw_hl[:, b, n, :].bitcast(F32), ident[:, :])
                last.then_inc(cwT_ps, 1)

            def bias_sums(b):
                pe.wait_ge(cwT_done, b + 1)
                if b == 0:
                    pe.wait_ge(b2_lo_done, 1)
                nc.tensor.matmul(psum[:, CW_BANKS[b], :], b2_hi[:, :], cwT[:, b, :], start=True, stop=False)
                nc.tensor.matmul(psum[:, CW_BANKS[b], :], b2_lo[0:E, :], cwT[0:E, b, :], start=False, stop=True).then_inc(b2_ps, 1)

            def broadcast_cw(s, u, b, r):
                if b == 0:
                    pe.wait_ge(w_split, 2 * s + 4 if not isinstance(s, int) or s >= 2 * B else 4 * s + 4)
                if isinstance(s, int) and s < 2 * B:
                    if s != 1:
                        pe.wait_ge(acc_init, b + 1)
                    else:
                        pe.wait_ge(logit_done, B)
                if not isinstance(s, int) or s >= B:
                    pe.wait_ge(cwb_done, s - 1)
                nc.tensor.matmul(psum[:, CWB_BANKS[r], :], sel_e[u][:, :], cwT[:, b, :], start=True, stop=True).then_inc(cwb_ps, 1)

            def second(i, j, first=False):
                (u, b), r, m = place(j, first), j // MT % 2, j % MT
                pe.wait_ge(g_lo_done, PT_TILES * i + j + 1)
                if m == 0 and not (first and j < B * MT):
                    pe.wait_ge(y_cw_done, 2 * B * i + j // MT - 1)
                if m == 0 and b == 0:
                    pe.wait_ge(w_split, 4 * (2 * i + u) + 4)
                last = three(psum[:, Y_BANKS[r], :], w2_hi[u][:, m, :], w2_lo[u][:, m, :], g_hi[:, j % 4, :], g_lo[:, j % 4, :],
                             start=(m == 0), stop=(m == MT - 1))
                if m == MT - 1:
                    last.then_inc(y_ps, 1)

            def pair(i, first=False):
                for j in range(PT_TILES):
                    (u, b), m = place(j, first), j % MT
                    if first and j == 0:
                        pe.wait_ge(exp_done, HEADS * T)
                    if m == 0 and b == 0:
                        pe.wait_ge(w_split, 4 * (2 * i + u) + 2)
                    if not (first and j < 4):
                        pe.wait_ge(g_lo_done, PT_TILES * i + j - 3)
                    toks = slice(b * NT, (b + 1) * NT)
                    cols = slice(m * P, (m + 1) * P)
                    three(psum[:, j % 4, :], w1_hi[u][:, cols], w1_lo[u][:, cols],
                          x2_hi[:, toks, :].rearrange("p n t -> p (n t)"),
                          x2_lo[:, toks, :].rearrange("p n t -> p (n t)")).then_inc(h_ps, 1)
                    if first:
                        if j == 0:
                            attention_out(T - 1)
                        if j == 1:
                            xT2(2)
                        if j == 2:
                            transpose_cw(0)
                        if j == 3:
                            xT2(3)
                        if j == 4:
                            bias_sums(0)
                        if j == 4:
                            gate_logits(1)
                        if j == 10:
                            pe.wait_ge(cwb_done, 2)
                            transpose_cw(1)
                        if j == 12:
                            bias_sums(1)
                        if j in CWB_AT:
                            step = CWB_AT.index(j)
                            broadcast_cw(step, step % B, step // B, step % 2)
                    elif m == MT - 1:
                        broadcast_cw(2 * B * i + j // MT, u, b, b)
                    if j >= LAG:
                        second(i, j - LAG, first)
                    elif not first:
                        second(i - 1, j - LAG + PT_TILES)

            pair(0, first=True)
            with pe.Fori(1, PAIRS) as i:
                pair(i)
            for j in range(PT_TILES - LAG, PT_TILES):
                second(PAIRS - 1, j)
            pe.wait_ge(acc_done, STEPS - 1)
            pe.wait_ge(cwb_done, STEPS - 1)
            for n in range(NT):
                last = nc.tensor.transpose(fin_psum(0, 0, NT)[:, n, :], acc[:, 0, n * P:(n + 1) * P], ident[:, :])
            last.then_inc(fin_ps, 1)
            for n in range(NT):
                nc.tensor.matmul(psum[:, n, 0:D], acc[:, 1, n * P:(n + 1) * P], ident[:, :], start=True, stop=False)
            for f in (1, 2):
                _, n0, n1 = FIN_PARTS[f]
                pe.wait_ge(y_cw_done, STEPS - 1 + f)
                for n in range(n0, n1):
                    last = nc.tensor.matmul(psum[:, n, 0:D], y_cw[:, 1, n * P:(n + 1) * P], ident[:, :], start=False, stop=True)
                last.then_inc(fin_ps, 1)


INPUTS = ["x", "ctx_1024", "g_xattn", "g_ffn", "L0_xattn_Wq", "L0_xattn_Wk", "L0_xattn_Wv", "L0_xattn_Wo", "L0_xattn_bo",
          "L0_ffn_w_gate", "L0_ffn_W1", "L0_ffn_b1", "L0_ffn_W2", "L0_ffn_b2"]


def kernel(**inputs):
    import numpy as np
    import concourse.bacc as bacc
    from concourse.bass_utils import run_bass_kernel_spmd

    nc = bacc.Bacc("TRN2", target_bir_lowering=False, num_devices=1)
    arrays, args = {}, []
    for name in INPUTS:
        a = np.ascontiguousarray(inputs[name])
        arrays[f"in_{name}"] = a
        args.append(nc.dram_tensor(f"in_{name}", a.shape, mybir.dt.from_np(a.dtype), kind="ExternalInput").ap())
    out = nc.dram_tensor("out_x", arrays["in_x"].shape, F32, kind="ExternalOutput").ap()
    flamingo_block(nc, *args, out)
    return run_bass_kernel_spmd(nc, [arrays], core_ids=[0]).results[0]["out_x"]
```

```python
from contextlib import ExitStack

import concourse.bass as bass
from concourse import mybir

F32 = mybir.dt.float32
F32R = mybir.dt.float32r
ALU = mybir.AluOpType
ACT = mybir.ActivationFunctionType
AX_X = mybir.AxisListType.X

P = 128
HEADS = 8
EPS = 1e-5
JUNK = -3.0e38
FOUND = 3.0e38
EULER = 2.718281828459045


def flamingo_block(nc, x, ctx_in, g_xattn, g_ffn, Wq, Wk, Wv, Wo, bo, w_gate, W1, b1, W2, b2, out):
    B, S, D = x.shape
    M = ctx_in.shape[1]
    INNER = Wq.shape[1]
    HD = INNER // HEADS
    E, _, HID = W1.shape
    assert D == P and HD == 64 and E == 8 and HID % P == 0 and S % P == 0
    NT = S // P
    T = B * NT
    J = INNER // P
    HM = HEADS * M
    HH = HM // 2
    CH = -(-HM // P)
    HMP = CH * P
    MT = HID // P
    STEPS = E * B
    LAG = 3
    PAIRS = E // 2
    PT_TILES = 2 * B * MT
    BW = 2 * P
    GT = 2

    with ExitStack() as stack:
        def sb(name, shape, dt=F32):
            return stack.enter_context(nc.sbuf_tensor(name, shape, dt))

        def sem(name):
            return stack.enter_context(nc.semaphore(name))

        psum = stack.enter_context(nc.psum_tensor("psum", [P, 8, 512], F32))
        psum_flat = psum[:, :, :].rearrange("p b n -> p (b n)")

        x_sb = sb("x_sb", [P, B, NT, D])
        ctx_sb = sb("ctx_sb", [M, B, D])
        wq_sb = sb("wq_sb", [P, INNER])
        wk_sb = sb("wk_sb", [P, INNER])
        wv_sb = sb("wv_sb", [P, INNER])
        wo_sb = sb("wo_sb", [P, J, D])
        bo_sb = sb("bo_sb", [P, D])
        gates_in = sb("gates_in", [P, 2])
        wg_sb = sb("wg_sb", [E, D])
        b1_sb = sb("b1_sb", [E * MT, P])
        b2_sb = sb("b2_sb", [E, D])
        w1_sb = sb("w1_sb", [P, E, HID])
        w2_sb = sb("w2_sb", [P, E, MT, D])
        ident = sb("ident", [P, P])
        minus_half = sb("minus_half", [P, T])
        euler = sb("euler", [P, NT, E])
        tanh_g = sb("tanh_g", [P, 2])
        tbo = sb("tbo", [P, D])
        wqT = sb("wqT", [P, J, D])
        ctxT = sb("ctxT", [P, B * M])
        kT = sb("kT", [P, J, B * M])
        v_blocks = sb("v_blocks", [P, B * J * BW + BW])
        a_hi = sb("a_hi", [P, B, HEADS, M], F32R)
        a_lo = sb("a_lo", [P, B, HEADS, M], F32R)
        vo_hl = sb("vo_hl", [P, B, CH, 2, D], F32R)
        wg_hi = sb("wg_hi", [P, E], F32R)
        wg_lo = sb("wg_lo", [P, E], F32R)
        b1T = sb("b1T", [P, E * MT])
        b2_hi = sb("b2_hi", [E, D], F32R)
        b2_lo = sb("b2_lo", [E, D], F32R)
        bn1 = sb("bn1", [P, T, 6])
        mv1 = sb("mv1", [P, T, 2])
        ve1 = sb("ve1", [P, T])
        rstd1 = sb("rstd1", [P, T])
        xb = sb("xb", [P, T, D])
        xn1 = sb("xn1", [P, T, D])
        xnT_hi = sb("xnT_hi", [P, T, P], F32R)
        xnT_lo = sb("xnT_lo", [P, T, P], F32R)
        smax = sb("smax", [P, 2, HEADS])
        ssum = sb("ssum", [P, 2, HEADS])
        srec = sb("srec", [P, 2, HEADS])
        prob = sb("prob", [P, 2, HMP])
        pT_hi = [sb(f"pT_hi{u}", [P, HMP], F32R) for u in range(2)]
        pT_lo = [sb(f"pT_lo{u}", [P, HMP], F32R) for u in range(2)]
        x1 = sb("x1", [P, T, D])
        bn2 = sb("bn2", [P, T, 6])
        mv2 = sb("mv2", [P, T, 2])
        ve2 = sb("ve2", [P, T])
        rstd2 = sb("rstd2", [P, T])
        xn2 = xn1
        x2_hi = sb("x2_hi", [P, T, P], F32R)
        x2_lo = sb("x2_lo", [P, T, P], F32R)
        logit = sb("logit", [P, B, NT, E + 6])
        top8 = sb("top8", [P, B, NT, 8])
        best = sb("best", [P, B, NT, 8])
        found = sb("found", [P, B, NT, E + 6])
        gd = sb("gd", [P, B, NT, E])
        gexp = sb("gexp", [P, B, NT, E])
        gsum = sb("gsum", [P, B, NT])
        grec = sb("grec", [P, B, NT])
        gscale = sb("gscale", [P, B, NT])
        gpick = sb("gpick", [P, B, NT, E])
        cw = sb("cw", [P, B, NT, E])
        cwT = sb("cwT", [E, B, S])
        cwT_hi = sb("cwT_hi", [E, S], F32R)
        cwT_lo = sb("cwT_lo", [E, S], F32R)
        b1_e = [sb(f"b1_e{u}", [P, MT]) for u in range(2)]
        cwb = sb("cwb", [P, 4, S])
        w1_hi = [sb(f"w1_hi{u}", [P, HID], F32R) for u in range(2)]
        w1_lo = [sb(f"w1_lo{u}", [P, HID], F32R) for u in range(2)]
        w2_hi = [sb(f"w2_hi{u}", [P, MT, D], F32R) for u in range(2)]
        w2_lo = [sb(f"w2_lo{u}", [P, MT, D], F32R) for u in range(2)]
        g_hi = sb("g_hi", [P, 4, S], F32R)
        g_lo = sb("g_lo", [P, 4, S], F32R)
        y_cw = sb("y_cw", [P, 2, S])
        acc = sb("acc", [P, B, S])
        fin = sb("fin", [P, B, NT * D])

        SC = [psum[:, 2 * u:2 * u + 2, 0:HH].rearrange("p b (h m) -> p b h m", m=M) for u in range(2)]
        PT = psum_flat[:, 4 * 512:4 * 512 + HMP]
        VO_PS = [psum_flat[:, bank * 512:bank * 512 + HMP] for bank in (4, 6)]
        AO = psum[:, 6, 0:2 * D].rearrange("p (w d) -> p w d", w=2)
        X_BANK = 7
        GATE_COL = 384
        SMALL_BANK = 6
        CW_BANKS = (6, 7)
        Y_BANKS = (4, 5)
        FIN_PARTS = ((0, 0, NT), (1, 0, NT // 2), (1, NT // 2, NT))

        def fin_psum(b, n0, n1):
            if b == 0:
                return psum[:, 6, :].rearrange("p (n d) -> p n d", d=D)
            return psum[:, n0:n1, 0:D]

        cw_rows = nc.dram_tensor("cw_rows", (B, E, S), F32, kind="Internal").ap()

        d_ctx, d_wq, d_wk, d_wv, d_wo = sem("d_ctx"), sem("d_wq"), sem("d_wk"), sem("d_wv"), sem("d_wo")
        d_x = [sem(f"d_x{b}") for b in range(B)]
        d_bo, d_g, d_wg, d_b1, d_b2 = sem("d_bo"), sem("d_g"), sem("d_wg"), sem("d_b1"), sem("d_b2")
        d_w1 = [sem(f"d_w1_{i}") for i in range(2)]
        d_w2 = [sem(f"d_w2_{i}") for i in range(2)]
        d_rows = [sem(f"d_rows{b}") for b in range(B)]
        d_cwb = [sem(f"d_cwb{k}") for k in range(4)]
        d_out = sem("d_out")
        ident_zero, ident_done = sem("ident_zero"), sem("ident_done")
        consts_done = sem("consts_done")
        vzero_done = sem("vzero_done")
        wqT_ps, wqT_done = sem("wqT_ps"), sem("wqT_done")
        ctxT_ps, ctxT_done = sem("ctxT_ps"), sem("ctxT_done")
        small_ps, small_done = sem("small_ps"), sem("small_done")
        wg_hi_done, wg_lo_done, b2_hi_done, b2_lo_done = sem("wg_hi_done"), sem("wg_lo_done"), sem("b2_hi_done"), sem("b2_lo_done")
        kT_ps, kT_done, vT_ps, v_done = sem("kT_ps"), sem("kT_done"), sem("vT_ps"), sem("v_done")
        a_ps, a_hi_done, a_lo_done = sem("a_ps"), sem("a_hi_done"), sem("a_lo_done")
        vo_ps, vo_hi_done, vo_lo_done = sem("vo_ps"), sem("vo_hi_done"), sem("vo_lo_done")
        tanh_done, tbo_done, xb_done = sem("tanh_done"), sem("tbo_done"), sem("xb_done")
        bn1_done, mv1_done, ve1_done, rstd1_done, xn1_done = sem("bn1_done"), sem("mv1_done"), sem("ve1_done"), sem("rstd1_done"), sem("xn1_done")
        xT1_ps, xT1_hi_done, xT1_lo_done = sem("xT1_ps"), sem("xT1_hi_done"), sem("xT1_lo_done")
        sc_ps, smax_done, exp_done = sem("sc_ps"), sem("smax_done"), sem("exp_done")
        srec_done, norm_done = sem("srec_done"), sem("norm_done")
        pT_ps, pT_hi_done, pT_lo_done = sem("pT_ps"), sem("pT_hi_done"), sem("pT_lo_done")
        x1_part_done = sem("x1_part_done")
        ao_ps, x1_done, bn2_done, mv2_done = sem("ao_ps"), sem("x1_done"), sem("bn2_done"), sem("mv2_done")
        ve2_done, rstd2_done, xn2_done = sem("ve2_done"), sem("rstd2_done"), sem("xn2_done")
        xT2_ps, x2_hi_done, x2_lo_done = sem("xT2_ps"), sem("x2_hi_done"), sem("x2_lo_done")
        gate_ps, logit_done, top8_done, best_done = sem("gate_ps"), sem("logit_done"), sem("top8_done"), sem("best_done")
        found_done, gd_done, gsum_done = sem("found_done"), sem("gd_done"), sem("gsum_done")
        gexp0_done, gexp1_done = sem("gexp0_done"), sem("gexp1_done")
        grec_done, gscale_done, gpick_done, cw_done = sem("grec_done"), sem("gscale_done"), sem("gpick_done"), sem("cw_done")
        cwT_ps, cwT_done, cwT_hi_done, cwT_lo_done = sem("cwT_ps"), sem("cwT_done"), sem("cwT_hi_done"), sem("cwT_lo_done")
        b2_ps, acc_init = sem("b2_ps"), sem("acc_init")
        w_hi_done, w_hi_seen, w_split = sem("w_hi_done"), sem("w_hi_seen"), sem("w_split")
        h_ps, gelu_done, g_hi_done, g_lo_done = sem("h_ps"), sem("gelu_done"), sem("g_hi_done"), sem("g_lo_done")
        y_ps, y_cw_done, acc_done = sem("y_ps"), sem("y_cw_done"), sem("acc_done")
        fin_ps, fin_done = sem("fin_ps"), sem("fin_done")

        A_BANKS = (0, 1, 4, 5)

        def a_psum(bank):
            return psum[:, A_BANKS[bank], 0:2 * B * M].rearrange("p (c b m) -> p b c m", c=2, b=B)

        def a_view(t, bank):
            first = 4 * (bank % 2) + bank // 2
            return t[:, :, first:first + 3:2, :]

        block = stack.enter_context(nc.Block())

        def place(j, first):
            step = j // MT
            return (step % B, step // B) if first else (step // B, step % B)

        CWT_AT, ACC_AT = (2, 12), (5, 15)

        @block.sync
        def _(sp):
            sp.dma_start(ctx_sb[:, :, :], ctx_in.rearrange("b m d -> m b d")).then_inc(d_ctx, 16)
            sp.dma_start(wk_sb[:, :], Wk).then_inc(d_wk, 16)
            sp.dma_start(x_sb[:, 0, :, :], x[0].rearrange("(p n) d -> p n d", n=NT)).then_inc(d_x[0], 16)
            sp.dma_start(wo_sb[:, :, :], Wo.rearrange("(j p) d -> p j d", p=P)).then_inc(d_wo, 16)
            sp.dma_start(x_sb[:, 1, :, :], x[1].rearrange("(p n) d -> p n d", n=NT)).then_inc(d_x[1], 16)
            sp.dma_start(wg_sb[:, :], w_gate).then_inc(d_wg, 16)
            sp.dma_start(b1_sb[:, :], b1.rearrange("e (m p) -> (e m) p", p=P)).then_inc(d_b1, 16)
            sp.dma_start(b2_sb[:, :], b2).then_inc(d_b2, 16)
            for i in range(2):
                half = slice(i * E // 2, (i + 1) * E // 2)
                sp.dma_start(w1_sb[:, half, :], W1[half].rearrange("e d h -> d e h")).then_inc(d_w1[i], 16)
                for e in range(i * E // 2, (i + 1) * E // 2):
                    sp.dma_start(w2_sb[:, e, :, :], W2[e].rearrange("(k p) d -> p k d", p=P)).then_inc(d_w2[i], 16)
            for s in range(STEPS):
                e, b = (s % B, s // B) if s < 2 * B else (s // B, s % B)
                if s in (0, B):
                    sp.wait_ge(cwT_done, b + 1)
                    sp.dma_start(cw_rows[b], cwT[:, b, :]).then_inc(d_rows[b], 16)
                    sp.wait_ge(d_rows[b], 16)
                if s >= 4:
                    sp.wait_ge(y_cw_done, s - 3)
                sp.dma_start(cwb[:, s % 4, :], cw_rows[b, e].partition_broadcast(P)).then_inc(d_cwb[s % 4], 16)
            for f, (b, n0, n1) in enumerate(FIN_PARTS):
                sp.wait_ge(fin_done, f + 1)
                cols = slice(n0 * D, n1 * D)
                sp.dma_start(out[b].rearrange("(p n) d -> p (n d)", n=NT)[:, cols], fin[:, b, cols]).then_inc(d_out, 16)
            sp.wait_ge(d_out, 16 * len(FIN_PARTS))

        @block.gpsimd
        def _(pool):
            nc.gpsimd.memset(ident[:, :], 0.0).then_inc(ident_zero, 1)
            pool.wait_ge(ident_zero, 1)
            nc.gpsimd.affine_select(out=ident[:, :], in_=ident[:, :], compare_op=ALU.not_equal, fill=1.0, base=0,
                                    pattern=[[-1, P]], channel_multiplier=1).then_inc(ident_done, 1)
            nc.gpsimd.memset(minus_half[:, :], -0.5).then_inc(consts_done, 1)
            nc.gpsimd.memset(v_blocks[:, :], 0.0).then_inc(vzero_done, 1)
            nc.gpsimd.memset(euler[:, :, :], EULER).then_inc(consts_done, 1)
            nc.gpsimd.memset(prob[:, :, HM:HMP], 0.0).then_inc(consts_done, 1)
            nc.gpsimd.memset(logit[:, :, :, E:E + 6], JUNK).then_inc(consts_done, 1)
            nc.gpsimd.memset(best[:, :, :, 2:8], JUNK).then_inc(consts_done, 1)
            def rstd1_of(b):
                tiles = slice(b * NT, (b + 1) * NT)
                pool.wait_ge(mv1_done, (b + 1) * NT)
                nc.gpsimd.tensor_scalar(ve1[:, tiles], mv1[:, tiles, 1], EPS, None, ALU.add).then_inc(ve1_done, 1)
                pool.wait_ge(ve1_done, b + 1)
                if b == 0:
                    pool.wait_ge(consts_done, 5)
                nc.gpsimd.tensor_tensor(rstd1[:, tiles], ve1[:, tiles], minus_half[:, tiles], ALU.pow).then_inc(rstd1_done, 1)

            rstd1_of(0)
            pool.wait_ge(d_bo, 16)
            pool.wait_ge(tanh_done, 1)
            nc.gpsimd.tensor_scalar(tbo[:, :], bo_sb[:, :], tanh_g[:, 0:1], None, ALU.mult).then_inc(tbo_done, 1)
            pool.wait_ge(tbo_done, 1)
            for b in range(B):
                pool.wait_ge(d_x[b], 16)
                nc.gpsimd.tensor_tensor(xb[:, b * NT:(b + 1) * NT, :], x_sb[:, b, :, :],
                                        tbo[:, :].unsqueeze(1).to_broadcast([P, NT, D]), ALU.add).then_inc(xb_done, 1)
            rstd1_of(1)

            def w1_rest(e, u):
                pool.wait_ge(w_hi_done, 2 * e + 1)
                pool.sem_inc(w_hi_seen, 1)
                nc.gpsimd.tensor_tensor(w1_lo[u][:, :], w1_sb[:, e, :], w1_hi[u][:, :].bitcast(F32), ALU.subtract).then_inc(w_split, 1)
                nc.gpsimd.tensor_copy(b1_e[u][:, :], b1T[:, bass.ds(e * MT, MT)]).then_inc(w_split, 1)

            def w2_rest(e, u):
                pool.wait_ge(w_hi_done, 2 * e + 2)
                pool.sem_inc(w_hi_seen, 1)
                nc.gpsimd.tensor_tensor(w2_lo[u][:, :, :], w2_sb[:, e, :, :], w2_hi[u][:, :, :].bitcast(F32), ALU.subtract).then_inc(w_split, 1)

            def split_lo(e, u):
                w1_rest(e, u)
                w2_rest(e, u)

            def rstd2_of(q):
                tiles = slice(q * GT, (q + 1) * GT)
                pool.wait_ge(mv2_done, (q + 1) * GT)
                nc.gpsimd.tensor_scalar(ve2[:, tiles], mv2[:, tiles, 1], EPS, None, ALU.add).then_inc(ve2_done, 1)
                pool.wait_ge(ve2_done, q + 1)
                nc.gpsimd.tensor_tensor(rstd2[:, tiles], ve2[:, tiles], minus_half[:, tiles], ALU.pow).then_inc(rstd2_done, 1)

            for k in range(T):
                pool.wait_ge(srec_done, k + 1)
                p_k = prob[:, k % 2, 0:HM].rearrange("p (h m) -> p h m", m=M)
                nc.gpsimd.tensor_tensor(p_k, p_k, srec[:, k % 2, :].unsqueeze(2).to_broadcast([P, HEADS, M]),
                                        ALU.mult).then_inc(norm_done, 1)
                if k >= 4 and k % 2 == 0:
                    rstd2_of((k - 4) // 2)
                if k == 3:
                    pool.wait_ge(small_done, 1)
                    w1_rest(0, 0)
                if k == 4:
                    w2_rest(0, 0)
                if k == 6:
                    w1_rest(1, 1)
                if k == 7:
                    w2_rest(1, 1)
            rstd2_of(2)
            rstd2_of(3)
            pool.wait_ge(gd_done, B)
            nc.gpsimd.tensor_tensor(gexp[:, 1, :, :], euler[:, :, :], gd[:, 1, :, :], ALU.pow).then_inc(gexp1_done, 1)

            def add_y(s, r, b):
                pool.wait_ge(y_cw_done, s + 1)
                if isinstance(s, int) and s in (0, B):
                    pool.wait_ge(acc_init, s // B + 1)
                else:
                    pool.wait_ge(acc_done, s)
                nc.gpsimd.tensor_tensor(acc[:, b, :], acc[:, b, :], y_cw[:, r, :], ALU.add).then_inc(acc_done, 1)

            def expert(e, u, last=False):
                if not last:
                    split_lo(e + 1, 1 - u)
                add_y(B * e - 1, 1, 1)
                add_y(B * e, 0, 0)

            add_y(0, 0, 0)
            add_y(1, 1, 0)
            pool.wait_ge(gelu_done, 3 * MT)
            w1_rest(2, 0)
            add_y(2, 0, 1)
            w2_rest(2, 0)
            with pool.Fori(1, PAIRS - 1) as i:
                expert(2 * i, 0)
                expert(2 * i + 1, 1)
            expert(E - 2, 0)
            expert(E - 1, 1, last=True)

        @block.scalar
        def _(act):
            act.dma_start(gates_in[:, 0:1], g_xattn.partition_broadcast(P)).then_inc(d_g, 16)
            act.dma_start(gates_in[:, 1:2], g_ffn.partition_broadcast(P)).then_inc(d_g, 16)
            act.dma_start(wq_sb[:, :], Wq).then_inc(d_wq, 16)
            act.dma_start(wv_sb[:, :], Wv).then_inc(d_wv, 16)
            act.dma_start(bo_sb[:, :], bo.partition_broadcast(P)).then_inc(d_bo, 16)
            act.wait_ge(d_g, 32)
            nc.scalar.activation(tanh_g[:, :], gates_in[:, :], ACT.Tanh).then_inc(tanh_done, 1)
            for q in range(2):
                act.wait_ge(kT_ps, q + 1)
                nc.scalar.activation(kT[:, 2 * q:2 * q + 2, :], psum[:, q, 0:2 * B * M].rearrange("p (c n) -> p c n", c=2),
                                     ACT.Copy, scale=HD ** -0.5).then_inc(kT_done, 1)
            for bank in range(4):
                act.wait_ge(a_ps, bank + 1)
                nc.scalar.copy(a_view(a_hi, bank), a_psum(bank)).then_inc(a_hi_done, 1)
            def xT1_hi(b):
                act.wait_ge(xT1_ps, b + 1)
                nc.scalar.copy(xnT_hi[:, b * NT:(b + 1) * NT, :], psum[:, X_BANK, :].rearrange("p (n t) -> p n t", n=NT)).then_inc(xT1_hi_done, 1)

            def x2_high(q):
                act.wait_ge(xT2_ps, q + 1)
                nc.scalar.copy(x2_hi[:, q * GT:(q + 1) * GT, :], psum[:, X_BANK, 0:GT * P].rearrange("p (n t) -> p n t", n=GT)).then_inc(x2_hi_done, 1)

            xT1_hi(0)
            act.wait_ge(vzero_done, 1)
            act.wait_ge(vT_ps, 2)
            for b in range(B):
                for par in range(2):
                    rows = slice(par * HD, (par + 1) * HD)
                    at = b * J * BW + par * M
                    stride = BW + 2 * M - P
                    dst = v_blocks[rows, at:at + J * stride].rearrange("p (j c) -> p j c", c=stride)[:, :, 0:M]
                    for half in range(2):
                        src = psum[rows, 2 + half, 0:2 * B * M].rearrange("p (c b m) -> p c b m", c=2, b=B)
                        nc.scalar.copy(dst[:, 2 * half:2 * half + 2, :], src[:, :, b, :]).then_inc(v_done, 1)
            act.wait_ge(small_ps, 1)
            nc.scalar.copy(wg_hi[:, :], psum[:, SMALL_BANK, 320:320 + E]).then_inc(wg_hi_done, 1)
            nc.scalar.copy(b1T[:, :], psum[:, SMALL_BANK, 352:352 + E * MT]).then_inc(small_done, 1)

            act.wait_ge(d_b2, 16)
            nc.scalar.copy(b2_hi[:, :], b2_sb[:, :]).then_inc(b2_hi_done, 1)

            for k in range(T + 1):
                if k < T:
                    act.wait_ge(smax_done, k + 1)
                    if k >= 2:
                        act.wait_ge(pT_ps, k - 1)
                    else:
                        act.wait_ge(consts_done, 5)
                    for h in range(HEADS):
                        nc.scalar.activation(prob[:, k % 2, h * M:(h + 1) * M], SC[k % 2][:, h // 4, h % 4, :], ACT.Exp,
                                             bias=smax[:, k % 2, h:h + 1], accum_out=ssum[:, k % 2, h:h + 1]).then_inc(exp_done, 1)
                if k in (0, 2):
                    act.wait_ge(vo_ps, k // 2 + 1)
                    nc.scalar.copy(vo_hl[:, k // 2, :, 0, :], VO_PS[k // 2].rearrange("p (c d) -> p c d", d=D)).then_inc(vo_hi_done, 1)
                if k >= 1:
                    act.wait_ge(pT_ps, k)
                    if k >= 3:
                        act.wait_ge(ao_ps, k - 2)
                    nc.scalar.copy(pT_hi[(k - 1) % 2][:, :], PT).then_inc(pT_hi_done, 1)
                if k == 0:
                    xT1_hi(1)
                if k in (6, 7):
                    x2_high(k - 6)
            act.wait_ge(gd_done, 1)
            nc.scalar.activation(gexp[:, 0, :, :], gd[:, 0, :, :], ACT.Exp).then_inc(gexp0_done, 1)

            def start_acc(b):
                act.wait_ge(b2_ps, b + 1)
                nc.scalar.copy(acc[:, b, :], psum[:, CW_BANKS[b], :]).then_inc(acc_init, 1)

            def copy_cwT(b):
                act.wait_ge(cwT_ps, b + 1)
                nc.scalar.copy(cwT[:, b, :], psum[0:E, CW_BANKS[b], :]).then_inc(cwT_done, 1)
                if b >= 1:
                    act.wait_ge(b2_ps, b)
                nc.scalar.copy(cwT_hi[:, :], psum[0:E, CW_BANKS[b], :]).then_inc(cwT_hi_done, 1)

            def pair(i, first=False):
                for j in range(PT_TILES):
                    g, s, m = PT_TILES * i + j, 2 * B * i + j // MT, j % MT
                    u, b = place(j, first)
                    act.wait_ge(h_ps, g + 1)
                    nc.scalar.activation(psum[:, j % 4, :], psum[:, j % 4, :], ACT.Gelu,
                                         bias=b1_e[u][:, m:m + 1]).then_inc(gelu_done, 1)
                    act.wait_ge(gelu_done, g + 1)
                    nc.scalar.copy(g_hi[:, j % 4, :], psum[:, j % 4, :]).then_inc(g_hi_done, 1)
                    if first and j in (1, 4):
                        x2_high(2 if j == 1 else 3)
                    if first and j in CWT_AT:
                        copy_cwT(CWT_AT.index(j))
                    if first and j in ACC_AT:
                        start_acc(ACC_AT.index(j))

            pair(0, first=True)
            with act.Fori(1, PAIRS) as i:
                pair(i)

        @block.vector
        def _(dve):
            def stats1(b):
                dve.wait_ge(d_x[b], 16)
                for t in range(b * NT, (b + 1) * NT):
                    nc.vector.bn_stats(bn1[:, t, :], x_sb[:, b, t % NT, :]).then_inc(bn1_done, 1)
                for t in range(b * NT, (b + 1) * NT):
                    dve.wait_ge(bn1_done, t + 1)
                    nc.vector.bn_aggr(mv1[:, t, :], bn1[:, t, :]).then_inc(mv1_done, 1)

            def normalise1(b):
                dve.wait_ge(rstd1_done, b + 1)
                for t in range(b * NT, (b + 1) * NT):
                    nc.vector.tensor_scalar(xn1[:, t, :], x_sb[:, b, t % NT, :], mv1[:, t, 0:1], rstd1[:, t:t + 1],
                                            ALU.subtract, ALU.mult).then_inc(xn1_done, 1)

            def xT1_lo(b):
                tiles = slice(b * NT, (b + 1) * NT)
                dve.wait_ge(xT1_hi_done, b + 1)
                nc.vector.tensor_tensor(xnT_lo[:, tiles, :], psum[:, X_BANK, :].rearrange("p (n t) -> p n t", n=NT),
                                        xnT_hi[:, tiles, :].bitcast(F32), ALU.subtract).then_inc(xT1_lo_done, 1)

            def row_max(k):
                dve.wait_ge(sc_ps, k + 1)
                nc.vector.tensor_reduce(smax[:, k % 2, :].rearrange("p (b h) -> p b h", b=2), SC[k % 2], AX_X, ALU.max,
                                        negate=True).then_inc(smax_done, 1)

            def x1_tile(t):
                dve.wait_ge(ao_ps, t + 1)
                dve.wait_ge(xb_done, t // NT + 1)
                nc.vector.scalar_tensor_tensor(x1[:, t, :], AO[:, 0, :], tanh_g[:, 0:1], xb[:, t, :],
                                               ALU.mult, ALU.add).then_inc(x1_part_done, 1)
                dve.wait_ge(x1_part_done, t + 1)
                nc.vector.scalar_tensor_tensor(x1[:, t, :], AO[:, 1, :], tanh_g[:, 0:1], x1[:, t, :],
                                               ALU.mult, ALU.add).then_inc(x1_done, 1)

            def stats2(t):
                dve.wait_ge(x1_done, t + 1)
                nc.vector.bn_stats(bn2[:, t, :], x1[:, t, :]).then_inc(bn2_done, 1)
                dve.wait_ge(bn2_done, t + 1)
                nc.vector.bn_aggr(mv2[:, t, :], bn2[:, t, :]).then_inc(mv2_done, 1)

            def normalise2(q):
                dve.wait_ge(rstd2_done, q + 1)
                for t in range(q * GT, (q + 1) * GT):
                    nc.vector.tensor_scalar(xn2[:, t, :], x1[:, t, :], mv2[:, t, 0:1], rstd2[:, t:t + 1],
                                            ALU.subtract, ALU.mult).then_inc(xn2_done, 1)

            def x2_rest(q):
                tiles = slice(q * GT, (q + 1) * GT)
                dve.wait_ge(x2_hi_done, q + 1)
                nc.vector.tensor_tensor(x2_lo[:, tiles, :], psum[:, X_BANK, 0:GT * P].rearrange("p (n t) -> p n t", n=GT),
                                        x2_hi[:, tiles, :].bitcast(F32), ALU.subtract).then_inc(x2_lo_done, 1)

            def split_hi(e, u):
                nc.vector.tensor_copy(w1_hi[u][:, :], w1_sb[:, e, :]).then_inc(w_hi_done, 1)
                nc.vector.tensor_copy(w2_hi[u][:, :, :], w2_sb[:, e, :, :]).then_inc(w_hi_done, 1)

            dve.wait_ge(ctxT_ps, 1)
            nc.vector.tensor_copy(ctxT[:, :], psum[:, 7, 0:B * M]).then_inc(ctxT_done, 1)
            stats1(0)
            dve.wait_ge(wqT_ps, 1)
            nc.vector.tensor_copy(wqT[:, :, :], psum[:, 6, 0:J * D].rearrange("p (j d) -> p j d", j=J)).then_inc(wqT_done, 1)
            normalise1(0)
            for bank in range(4):
                dve.wait_ge(a_hi_done, bank + 1)
                nc.vector.tensor_tensor(a_view(a_lo, bank), a_psum(bank), a_view(a_hi, bank).bitcast(F32),
                                        ALU.subtract).then_inc(a_lo_done, 1)
            xT1_lo(0)
            stats1(1)
            row_max(0)

            for k in range(T + 1):
                if k >= 3:
                    x1_tile(k - 3)
                if k + 1 < T:
                    row_max(k + 1)
                if k == 0:
                    normalise1(1)
                if k < T:
                    dve.wait_ge(exp_done, HEADS * (k + 1))
                    nc.vector.reciprocal(srec[:, k % 2, :], ssum[:, k % 2, :]).then_inc(srec_done, 1)
                if k >= 3:
                    stats2(k - 3)
                if k in (5, 7):
                    normalise2((k - 5) // 2)
                if k in (0, 2):
                    dve.wait_ge(vo_hi_done, k // 2 + 1)
                    nc.vector.tensor_tensor(vo_hl[:, k // 2, :, 1, :], VO_PS[k // 2].rearrange("p (c d) -> p c d", d=D),
                                            vo_hl[:, k // 2, :, 0, :].bitcast(F32), ALU.subtract).then_inc(vo_lo_done, 1)
                if k >= 1:
                    dve.wait_ge(pT_hi_done, k)
                    nc.vector.tensor_tensor(pT_lo[(k - 1) % 2][:, :], PT, pT_hi[(k - 1) % 2][:, :].bitcast(F32),
                                            ALU.subtract).then_inc(pT_lo_done, 1)
                if k == 0:
                    dve.wait_ge(wg_hi_done, 1)
                    dve.wait_ge(small_done, 1)
                    nc.vector.tensor_tensor(wg_lo[:, :], psum[:, SMALL_BANK, 320:320 + E], wg_hi[:, :].bitcast(F32), ALU.subtract).then_inc(wg_lo_done, 1)
                    dve.wait_ge(b2_hi_done, 1)
                    nc.vector.tensor_tensor(b2_lo[:, :], b2_sb[:, :], b2_hi[:, :].bitcast(F32), ALU.subtract).then_inc(b2_lo_done, 1)
                if k == 0:
                    xT1_lo(1)
                if k == 2:
                    dve.wait_ge(d_w1[0], 16)
                    dve.wait_ge(d_w2[0], 16 * (E // 2))
                    split_hi(0, 0)
                if k == 3:
                    split_hi(1, 1)
                if k in (6, 7):
                    x2_rest(k - 6)

            def choose(b):
                dve.wait_ge(gate_ps, b + 1)
                nc.vector.tensor_copy(logit[:, b, :, 0:E], psum[:, X_BANK, GATE_COL:GATE_COL + NT * E].rearrange("p (n e) -> p n e", e=E)).then_inc(logit_done, 1)
                dve.wait_ge(logit_done, b + 1)
                for n in range(NT):
                    nc.vector.max(top8[:, b, n, :], logit[:, b, n, 0:E]).then_inc(top8_done, 1)
                dve.wait_ge(top8_done, (b + 1) * NT)
                nc.vector.tensor_tensor(gd[:, b, :, :], logit[:, b, :, 0:E], top8[:, b, :, 0:1].to_broadcast([P, NT, E]),
                                        ALU.subtract).then_inc(gd_done, 1)
                nc.vector.tensor_copy(best[:, b, :, 0:2], top8[:, b, :, 0:2]).then_inc(best_done, 1)
                dve.wait_ge(best_done, b + 1)
                for n in range(NT):
                    nc.vector.match_replace(found[:, b, n, :], best[:, b, n, :], logit[:, b, n, :], FOUND).then_inc(found_done, 1)

            def combine_weights(b):
                dve.wait_ge((gexp0_done, gexp1_done)[b], 1)
                nc.vector.tensor_reduce(gsum[:, b, :], gexp[:, b, :, :], AX_X, ALU.add).then_inc(gsum_done, 1)
                dve.wait_ge(found_done, (b + 1) * NT)
                nc.vector.scalar_tensor_tensor(gpick[:, b, :, :], found[:, b, :, 0:E], 0.5 * FOUND, gexp[:, b, :, :],
                                               ALU.is_ge, ALU.mult).then_inc(gpick_done, 1)
                dve.wait_ge(gsum_done, b + 1)
                nc.vector.reciprocal(grec[:, b, :], gsum[:, b, :]).then_inc(grec_done, 1)
                dve.wait_ge(grec_done, b + 1)
                nc.vector.tensor_scalar(gscale[:, b, :], grec[:, b, :], tanh_g[:, 1:2], None, ALU.mult).then_inc(gscale_done, 1)
                dve.wait_ge(gscale_done, b + 1)
                dve.wait_ge(gpick_done, b + 1)
                nc.vector.tensor_tensor(cw[:, b, :, :], gpick[:, b, :, :], gscale[:, b, :].unsqueeze(2).to_broadcast([P, NT, E]),
                                        ALU.mult).then_inc(cw_done, 1)

            def cwT_rest(b):
                dve.wait_ge(cwT_hi_done, b + 1)
                nc.vector.tensor_tensor(cwT_lo[:, :], psum[0:E, CW_BANKS[b], :], cwT_hi[:, :].bitcast(F32),
                                        ALU.subtract).then_inc(cwT_lo_done, 1)

            x1_tile(T - 2)
            stats2(T - 2)
            choose(0)
            normalise2(2)
            combine_weights(0)
            x1_tile(T - 1)
            stats2(T - 1)

            def weight_y(s, k):
                dve.wait_ge(y_ps, s + 1)
                r = k % 2
                dve.wait_ge(d_cwb[k], 16 * (s - k) // 4 + 16 if isinstance(s, int) else 4 * (s - k) + 16)
                if not isinstance(s, int) or s >= B:
                    dve.wait_ge(acc_done, s - 1)
                nc.vector.tensor_tensor(y_cw[:, r, :], psum[:, Y_BANKS[r], :], cwb[:, k, :], ALU.mult).then_inc(y_cw_done, 1)

            def pair(i, first=False, last=False):
                for j in range(PT_TILES):
                    g, s, u, m = PT_TILES * i + j, 2 * B * i + j // MT, j // (B * MT), j % MT
                    dve.wait_ge(g_hi_done, g + 1)
                    nc.vector.tensor_tensor(g_lo[:, j % 4, :], psum[:, j % 4, :], g_hi[:, j % 4, :].bitcast(F32),
                                            ALU.subtract).then_inc(g_lo_done, 1)
                    if first:
                        if j == 0:
                            x2_rest(2)
                        if j == 1:
                            normalise2(3)
                            cwT_rest(0)
                        if j == 3:
                            x2_rest(3)
                        if j == 5:
                            choose(1)
                        if j == 9:
                            combine_weights(1)
                        if j == 8:
                            weight_y(0, 0)
                        if j == 11:
                            weight_y(1, 1)
                        if j == 14:
                            weight_y(2, 2)
                        if j == 12:
                            cwT_rest(1)
                        if j == 12:
                            dve.wait_ge(h_ps, 3 * MT)
                            nc.vector.tensor_copy(w1_hi[0][:, :], w1_sb[:, 2, :]).then_inc(w_hi_done, 1)
                        if j == 14:
                            nc.vector.tensor_copy(w2_hi[0][:, :, :], w2_sb[:, 2, :, :]).then_inc(w_hi_done, 1)
                        continue
                    if m == LAG - 1:
                        weight_y(s - 1, (j // MT - 1) % 4)
                    if j % (B * MT) == LAG - 1 and not (last and u == 1):
                        split_hi(2 * i + u + 1, 1 - u)

            dve.wait_ge(d_w1[1], 16)
            dve.wait_ge(d_w2[1], 16 * (E // 2))
            pair(0, first=True)
            with dve.Fori(1, PAIRS - 1) as i:
                pair(i)
            pair(PAIRS - 1, last=True)

            def finish(f):
                b, n0, n1 = FIN_PARTS[f]
                dve.wait_ge(fin_ps, f + 1)
                nc.vector.tensor_tensor(fin[:, b, n0 * D:n1 * D].rearrange("p (n d) -> p n d", n=n1 - n0),
                                        fin_psum(b, n0, n1),
                                        x1[:, b * NT + n0:b * NT + n1, :], ALU.add).then_inc(fin_done, 1)

            dve.wait_ge(y_ps, STEPS)
            dve.wait_ge(d_cwb[3], 16 * PAIRS)
            dve.wait_ge(acc_done, STEPS - 2)
            for half in range(2):
                toks = slice(half * S // 2, (half + 1) * S // 2)
                nc.vector.tensor_tensor(y_cw[:, 1, toks], psum[:, Y_BANKS[1], toks], cwb[:, 3, toks], ALU.mult).then_inc(y_cw_done, 1)
            for f in range(3):
                finish(f)

        @block.tensor
        def _(pe):
            def xT1(b):
                pe.wait_ge(xn1_done, (b + 1) * NT)
                for n in range(NT):
                    last = nc.tensor.transpose(psum[:, X_BANK, n * P:(n + 1) * P], xn1[:, b * NT + n, :], ident[:, :])
                last.then_inc(xT1_ps, 1)

            def three(acc_out, hi, lo, r_hi, r_lo, start=True, stop=True):
                nc.tensor.matmul(acc_out, hi, r_hi, start=start, stop=False)
                nc.tensor.matmul(acc_out, hi, r_lo, start=False, stop=False)
                return nc.tensor.matmul(acc_out, lo, r_hi, start=False, stop=stop)

            def scores(k):
                b = k // NT
                pe.wait_ge(xT1_lo_done, b + 1)
                if k == 1:
                    pe.wait_ge(v_done, 8)
                if k >= 2:
                    pe.wait_ge(exp_done, HEADS * (k - 1))
                for half in range(2):
                    heads = slice(half * HEADS // 2, (half + 1) * HEADS // 2)
                    last = three(psum[:, 2 * (k % 2) + half, 0:HH], xnT_hi[:, k, :], xnT_lo[:, k, :],
                                 a_hi[:, b, heads, :].rearrange("p h m -> p (h m)"),
                                 a_lo[:, b, heads, :].rearrange("p h m -> p (h m)"))
                last.then_inc(sc_ps, 1)

            pe.wait_ge(ident_done, 1)
            pe.wait_ge(d_ctx, 16)
            for b in range(B):
                last = nc.tensor.transpose(psum[:, 7, b * M:(b + 1) * M], ctx_sb[:, b, :], ident[0:M, 0:M])
            last.then_inc(ctxT_ps, 1)

            def project_ctx(w_sb, d_w, ps, bank):
                pe.wait_ge(d_w, 16)
                for j in range(J):
                    last = nc.tensor.matmul(psum[:, bank + j // 2, (j % 2) * B * M:(j % 2 + 1) * B * M],
                                            w_sb[:, j * P:(j + 1) * P], ctxT[:, :], start=True, stop=True)
                    if j % 2:
                        last.then_inc(ps, 1)

            pe.wait_ge(ctxT_done, 1)
            project_ctx(wk_sb, d_wk, kT_ps, 0)
            pe.wait_ge(d_wq, 16)
            for j in range(J):
                last = nc.tensor.transpose(psum[:, 6, j * P:(j + 1) * P], wq_sb[:, j * P:(j + 1) * P], ident[:, :])
            last.then_inc(wqT_ps, 1)
            project_ctx(wv_sb, d_wv, vT_ps, 2)
            pe.wait_ge(kT_done, 2)
            pe.wait_ge(wqT_done, 1)
            for bank in range(4):
                parity, half = bank // 2, bank % 2
                rows = slice(parity * HD, (parity + 1) * HD)
                for c in range(2):
                    last = nc.tensor.matmul(psum[:, A_BANKS[bank], c * B * M:(c + 1) * B * M], wqT[rows, 2 * half + c, :],
                                            kT[rows, 2 * half + c, :], start=True, stop=True)
                last.then_inc(a_ps, 1)
            xT1(0)
            pe.wait_ge(d_b1, 16)
            pe.wait_ge(d_wg, 16)
            nc.tensor.transpose(psum[:, SMALL_BANK, 320:320 + E], wg_sb[:, :], ident[0:E, 0:E])
            nc.tensor.transpose(psum[:, SMALL_BANK, 352:352 + E * MT], b1_sb[:, :], ident[0:E * MT, 0:E * MT]).then_inc(small_ps, 1)
            pe.wait_ge(a_lo_done, 4)
            scores(0)

            def fold_vo(b):
                for c in range(CH):
                    js = [j for j in (c - 1, c) if 0 <= j < J]
                    for j in js:
                        at = (b * J + j) * BW + (c - j) * P
                        last = nc.tensor.matmul(VO_PS[b][:, c * P:(c + 1) * P], v_blocks[:, at:at + P], wo_sb[:, j, :],
                                                start=(j == js[0]), stop=(j == js[-1]))
                last.then_inc(vo_ps, 1)

            def transpose_probs(k):
                pe.wait_ge(norm_done, k + 1)
                if k >= 1:
                    pe.wait_ge(pT_lo_done, k)
                for c in range(CH):
                    cols = slice(c * P, (c + 1) * P)
                    last = nc.tensor.transpose(PT[:, cols], prob[:, k % 2, cols], ident[:, :])
                last.then_inc(pT_ps, 1)

            def attention_out(k):
                pe.wait_ge(pT_lo_done, k + 1)
                if k == 0:
                    pe.wait_ge(vo_lo_done, 2)
                else:
                    pe.wait_ge(x1_done, k)
                for c in range(CH):
                    cols, b = slice(c * P, (c + 1) * P), k // NT
                    both = (AO, pT_hi[k % 2][:, cols], vo_hl[:, b, c, :, :])
                    first_part = (AO[:, 0, :], pT_lo[k % 2][:, cols], vo_hl[:, b, c, 0, :])
                    order = (both, first_part) if c < CH - 1 else (first_part, both)
                    for i, operands in enumerate(order):
                        last = nc.tensor.matmul(*operands, start=(c == 0 and i == 0), stop=(c == CH - 1 and i == 1))
                last.then_inc(ao_ps, 1)

            def xT2(q):
                pe.wait_ge(xn2_done, (q + 1) * GT)
                if q >= 1:
                    pe.wait_ge(x2_lo_done, q)
                if q >= 2:
                    pe.wait_ge(logit_done, 1)
                for n in range(GT):
                    last = nc.tensor.transpose(psum[:, X_BANK, n * P:(n + 1) * P], xn2[:, q * GT + n, :], ident[:, :])
                last.then_inc(xT2_ps, 1)

            def gate_logits(b):
                pe.wait_ge(x2_lo_done, (b + 1) * NT // GT)
                for n in range(NT):
                    t = b * NT + n
                    last = three(psum[:, X_BANK, GATE_COL + n * E:GATE_COL + (n + 1) * E], x2_hi[:, t, :], x2_lo[:, t, :],
                                 wg_hi[:, :], wg_lo[:, :])
                last.then_inc(gate_ps, 1)

            for k in range(T + 1):
                if k + 1 < T:
                    scores(k + 1)
                if k == 0:
                    pe.wait_ge(d_wo, 16)
                    fold_vo(0)
                    pe.wait_ge(xT1_lo_done, 1)
                    xT1(1)
                if k == 3:
                    attention_out(0)
                if k >= 1:
                    if k == 1:
                        pe.wait_ge(vo_lo_done, 1)
                    transpose_probs(k - 1)
                if k == 1:
                    pe.wait_ge(small_done, 1)
                    pe.wait_ge(wg_lo_done, 1)
                    pe.wait_ge(xT1_lo_done, 2)
                    fold_vo(1)
                if k >= 3:
                    attention_out(k - 2)
                if k == T:
                    gate_logits(0)
                if k in (5, 7):
                    xT2((k - 5) // 2)

            def transpose_cw(b):
                pe.wait_ge(cw_done, b + 1)
                if b == 0:
                    pe.wait_ge(x1_done, T)
                for n in range(NT):
                    last = nc.tensor.transpose(psum[0:E, CW_BANKS[b], n * P:(n + 1) * P], cw[:, b, n, :], ident[:, :])
                last.then_inc(cwT_ps, 1)

            def bias_sums(b):
                pe.wait_ge(cwT_lo_done, b + 1)
                if b == 0:
                    pe.wait_ge(b2_lo_done, 1)
                three(psum[:, CW_BANKS[b], :], b2_hi[:, :], b2_lo[:, :], cwT_hi[:, :], cwT_lo[:, :]).then_inc(b2_ps, 1)

            def second(i, j, first=False):
                (u, b), r, m = place(j, first), j // MT % 2, j % MT
                pe.wait_ge(g_lo_done, PT_TILES * i + j + 1)
                if m == 0 and not (first and j < B * MT):
                    pe.wait_ge(y_cw_done, 2 * B * i + j // MT - 1)
                if m == 0 and b == 0:
                    pe.wait_ge(w_split, 3 * (2 * i + u) + 3)
                last = three(psum[:, Y_BANKS[r], :], w2_hi[u][:, m, :], w2_lo[u][:, m, :], g_hi[:, j % 4, :], g_lo[:, j % 4, :],
                             start=(m == 0), stop=(m == MT - 1))
                if m == MT - 1:
                    last.then_inc(y_ps, 1)

            def pair(i, first=False):
                for j in range(PT_TILES):
                    (u, b), m = place(j, first), j % MT
                    if first and j == 0:
                        pe.wait_ge(exp_done, HEADS * T)
                    if m == 0 and b == 0:
                        pe.wait_ge(w_split, 3 * (2 * i + u) + 2)
                    if not (first and j < 4):
                        pe.wait_ge(g_lo_done, PT_TILES * i + j - 3)
                    toks = slice(b * NT, (b + 1) * NT)
                    cols = slice(m * P, (m + 1) * P)
                    three(psum[:, j % 4, :], w1_hi[u][:, cols], w1_lo[u][:, cols],
                          x2_hi[:, toks, :].rearrange("p n t -> p (n t)"),
                          x2_lo[:, toks, :].rearrange("p n t -> p (n t)")).then_inc(h_ps, 1)
                    if first:
                        if j == 0:
                            attention_out(T - 1)
                        if j == 1:
                            xT2(2)
                        if j == CWT_AT[0]:
                            transpose_cw(0)
                        if j == 4:
                            xT2(3)
                        if j in ACC_AT:
                            bias_sums(ACC_AT.index(j))
                        if j == 6:
                            gate_logits(1)
                        if j == CWT_AT[1]:
                            transpose_cw(1)
                    if j >= LAG:
                        second(i, j - LAG, first)
                    elif not first:
                        second(i - 1, j - LAG + PT_TILES)

            pair(0, first=True)
            with pe.Fori(1, PAIRS) as i:
                pair(i)
            for j in range(PT_TILES - LAG, PT_TILES):
                second(PAIRS - 1, j)
            pe.wait_ge(acc_done, STEPS - 1)
            for n in range(NT):
                last = nc.tensor.transpose(fin_psum(0, 0, NT)[:, n, :], acc[:, 0, n * P:(n + 1) * P], ident[:, :])
            last.then_inc(fin_ps, 1)
            for n in range(NT):
                nc.tensor.matmul(psum[:, n, 0:D], acc[:, 1, n * P:(n + 1) * P], ident[:, :], start=True, stop=False)
            for f in (1, 2):
                _, n0, n1 = FIN_PARTS[f]
                pe.wait_ge(y_cw_done, STEPS - 1 + f)
                for n in range(n0, n1):
                    last = nc.tensor.matmul(psum[:, n, 0:D], y_cw[:, 1, n * P:(n + 1) * P], ident[:, :], start=False, stop=True)
                last.then_inc(fin_ps, 1)


INPUTS = ["x", "ctx_1024", "g_xattn", "g_ffn", "L0_xattn_Wq", "L0_xattn_Wk", "L0_xattn_Wv", "L0_xattn_Wo", "L0_xattn_bo",
          "L0_ffn_w_gate", "L0_ffn_W1", "L0_ffn_b1", "L0_ffn_W2", "L0_ffn_b2"]


def kernel(**inputs):
    import numpy as np
    import concourse.bacc as bacc
    from concourse.bass_utils import run_bass_kernel_spmd

    nc = bacc.Bacc("TRN2", target_bir_lowering=False, num_devices=1)
    arrays, args = {}, []
    for name in INPUTS:
        a = np.ascontiguousarray(inputs[name])
        arrays[f"in_{name}"] = a
        args.append(nc.dram_tensor(f"in_{name}", a.shape, mybir.dt.from_np(a.dtype), kind="ExternalInput").ap())
    out = nc.dram_tensor("out_x", arrays["in_x"].shape, F32, kind="ExternalOutput").ap()
    flamingo_block(nc, *args, out)
    return run_bass_kernel_spmd(nc, [arrays], core_ids=[0]).results[0]["out_x"]
```
